# Optimizing a Trainium2 kernel written in Bass

```python
import numpy as np
import jax
import jax.numpy as jnp

def _softmax(x, axis=-1):
    return jax.nn.softmax(x, axis=axis)

def _gelu(x):
    return jax.nn.gelu(x, approximate=True)

def _silu(x):
    return jax.nn.silu(x)

def _sigmoid(x):
    return jax.nn.sigmoid(x)

def _layernorm(x, axis=-1, eps=1e-05):
    m = jnp.mean(x, axis=axis, keepdims=True)
    v = jnp.var(x, axis=axis, keepdims=True)
    return (x - m) / jnp.sqrt(v + eps)

def _scatter_add(tgt, idx, src, axis=0):
    return tgt.at[idx].add(src)

def _segment_sum(src, seg, n):
    return jax.ops.segment_sum(src, seg, n)
kernel_name = 'mk_vit_tower_cls_d1_tok_img1024_r4_6076c2'

def setup_inputs(seed: int=0):
    np.random.seed(seed)
    _w = jnp.asarray

    def _rec_inputs():
        import jax
        import jax.numpy as jnp
        _rk = jax.random.key(seed)
        x = -4.65018e-05 + 0.999886 * jax.random.normal(jax.random.fold_in(_rk, 1), (32, 3, 96, 96), jnp.float32)
        cls_tok = 0.02 * jax.random.normal(jax.random.fold_in(_rk, 5), (1, 1, 256), jnp.float32)
        return (x, cls_tok)
    x, cls_tok = _rec_inputs()

    def _L0_tok_setup():
        import jax, jax.numpy as jnp
        import numpy as np
        P = 16
        key = jax.random.key(seed)
        k1, k2, k3 = jax.random.split(key, 3)
        B, C, H, W_ = (64, 3, 128, 128)
        D = 256
        x = jax.random.normal(k1, (B, C, H, W_), dtype=jnp.float32)
        W = jax.random.normal(k2, (C * P * P, D), dtype=jnp.float32) * (1.0 / np.sqrt(C * P * P))
        b = jax.random.normal(k3, (D,), dtype=jnp.float32) * 0.01
        return {'x': x, 'W': W, 'b': b}
    _L0_tok_all = _L0_tok_setup()
    _L0_tok_in = {k: v for k, v in _L0_tok_all.items() if k in ('W', 'b')}
    del _L0_tok_all

    def _L0_attn_setup():
        import jax, jax.numpy as jnp
        import numpy as np
        HEADS = 16

        def _binarize(W):
            alpha = jnp.mean(jnp.abs(W), axis=tuple(range(1, W.ndim)), keepdims=True)
            B = W + jax.lax.stop_gradient(jnp.sign(W) - W)
            return alpha * B

        def _binlinear(x, W, b):
            Wb = _binarize(W)
            return jnp.einsum('btc,oc->bto', x, Wb) + b
        key = jax.random.key(seed)
        ks = jax.random.split(key, 9)
        dim = 256
        B, T = (4, 512)
        inp = {'x': jax.random.normal(ks[0], (B, T, dim), jnp.float32), 'Wq': jax.random.normal(ks[1], (dim, dim), jnp.float32) * 0.02, 'bq': jax.random.normal(ks[2], (dim,), jnp.float32) * 0.02, 'Wk': jax.random.normal(ks[3], (dim, dim), jnp.float32) * 0.02, 'bk': jax.random.normal(ks[4], (dim,), jnp.float32) * 0.02, 'Wv': jax.random.normal(ks[5], (dim, dim), jnp.float32) * 0.02, 'bv': jax.random.normal(ks[6], (dim,), jnp.float32) * 0.02, 'Wp': jax.random.normal(ks[7], (dim, dim), jnp.float32) * 0.02, 'bp': jax.random.normal(ks[8], (dim,), jnp.float32) * 0.02}
        return inp
    _L0_attn_all = _L0_attn_setup()
    _L0_attn_in = {k: v for k, v in _L0_attn_all.items() if k in ('Wq', 'bq', 'Wk', 'bk', 'Wv', 'bv', 'Wp', 'bp')}
    del _L0_attn_all

    def _L0_ffn_setup():
        import jax, jax.numpy as jnp
        import numpy as np
        TOP_K = 4
        N_GROUP = 4
        TOPK_GROUP = 2
        ROUTED_SCALING = 2.5

        def _route(x, gate_weight):
            scores = jax.nn.sigmoid(x @ gate_weight.T)
            T, E = scores.shape
            gs = E // N_GROUP
            top2, _ = jax.lax.top_k(scores.reshape(T, N_GROUP, gs), 2)
            group_scores = top2.sum(-1)
            _, gidx = jax.lax.top_k(group_scores, TOPK_GROUP)
            gmask = jax.nn.one_hot(gidx, N_GROUP, dtype=jnp.float32).sum(1)
            smask = jnp.repeat(gmask, gs, axis=1) > 0.5
            masked = jnp.where(smask, scores, 0.0)
            topk_idx = jax.lax.top_k(masked, TOP_K)[1]
            topk_w = jnp.take_along_axis(scores, topk_idx, axis=1)
            topk_w = topk_w / (topk_w.sum(-1, keepdims=True) + 1e-20)
            topk_w = topk_w * ROUTED_SCALING
            combine = jnp.zeros((T, E), jnp.float32).at[jnp.arange(T)[:, None], topk_idx].add(topk_w)
            return combine
        key = jax.random.key(seed)
        ks = jax.random.split(key, 6)
        B, S, H = (2, 256, 256)
        E, I, Is = (16, 128, 512)
        g = lambda k, shape, scale: jax.random.normal(k, shape, dtype=jnp.float32) * scale
        return {'hidden_states': g(ks[0], (B, S, H), 1.0), 'gate_weight': g(ks[1], (E, H), 0.02), 'expert_up': g(ks[2], (E, H, I), 0.02), 'expert_down': g(ks[3], (E, I, H), 0.02), 'shared_up': g(ks[4], (H, Is), 0.02), 'shared_down': g(ks[5], (Is, H), 0.02)}
    _L0_ffn_all = _L0_ffn_setup()
    _L0_ffn_in = {k: v for k, v in _L0_ffn_all.items() if k in ('gate_weight', 'expert_up', 'expert_down', 'shared_up', 'shared_down')}
    del _L0_ffn_all
    return {'x': x, 'cls_tok': cls_tok, 'L0_tok_W': _L0_tok_in['W'], 'L0_tok_b': _L0_tok_in['b'], 'L0_attn_Wq': _L0_attn_in['Wq'], 'L0_attn_bq': _L0_attn_in['bq'], 'L0_attn_Wk': _L0_attn_in['Wk'], 'L0_attn_bk': _L0_attn_in['bk'], 'L0_attn_Wv': _L0_attn_in['Wv'], 'L0_attn_bv': _L0_attn_in['bv'], 'L0_attn_Wp': _L0_attn_in['Wp'], 'L0_attn_bp': _L0_attn_in['bp'], 'L0_ffn_gate_weight': _L0_ffn_in['gate_weight'], 'L0_ffn_expert_up': _L0_ffn_in['expert_up'], 'L0_ffn_expert_down': _L0_ffn_in['expert_down'], 'L0_ffn_shared_up': _L0_ffn_in['shared_up'], 'L0_ffn_shared_down': _L0_ffn_in['shared_down']}

def reference(x, cls_tok, L0_tok_W, L0_tok_b, L0_attn_Wq, L0_attn_bq, L0_attn_Wk, L0_attn_bk, L0_attn_Wv, L0_attn_bv, L0_attn_Wp, L0_attn_bp, L0_ffn_gate_weight, L0_ffn_expert_up, L0_ffn_expert_down, L0_ffn_shared_up, L0_ffn_shared_down):
    import jax
    import jax.numpy as jnp

    def _L0_tok_ref(x, W, b):
        import jax, jax.numpy as jnp
        import numpy as np
        P = 16
        B, C, H, W_ = x.shape
        nh, nw = (H // P, W_ // P)
        patches = x.reshape(B, C, nh, P, nw, P)
        patches = patches.transpose(0, 2, 4, 1, 3, 5)
        patches = patches.reshape(B, nh * nw, C * P * P)
        return jnp.einsum('bnk,kd->bnd', patches, W) + b

    def _L0_attn_ref(x, Wq, bq, Wk, bk, Wv, bv, Wp, bp):
        import jax, jax.numpy as jnp
        import numpy as np
        HEADS = 16

        def _binarize(W):
            alpha = jnp.mean(jnp.abs(W), axis=tuple(range(1, W.ndim)), keepdims=True)
            B = W + jax.lax.stop_gradient(jnp.sign(W) - W)
            return alpha * B

        def _binlinear(x, W, b):
            Wb = _binarize(W)
            return jnp.einsum('btc,oc->bto', x, Wb) + b
        B, T, C = x.shape
        H = HEADS
        Dh = C // H
        scale = Dh ** (-0.5)

        def split_heads(t):
            return t.reshape(B, T, H, Dh).transpose(0, 2, 1, 3)
        q = split_heads(_binlinear(x, Wq, bq))
        k = split_heads(_binlinear(x, Wk, bk))
        v = split_heads(_binlinear(x, Wv, bv))
        att = jnp.einsum('bhtd,bhsd->bhts', q, k) * scale
        att = jax.nn.softmax(att, axis=-1)
        y = jnp.einsum('bhts,bhsd->bhtd', att, v)
        y = y.transpose(0, 2, 1, 3).reshape(B, T, C)
        return _binlinear(y, Wp, bp)

    def _L0_ffn_ref(hidden_states, gate_weight, expert_up, expert_down, shared_up, shared_down):
        import jax, jax.numpy as jnp
        import numpy as np
        TOP_K = 4
        N_GROUP = 4
        TOPK_GROUP = 2
        ROUTED_SCALING = 2.5

        def _route(x, gate_weight):
            scores = jax.nn.sigmoid(x @ gate_weight.T)
            T, E = scores.shape
            gs = E // N_GROUP
            top2, _ = jax.lax.top_k(scores.reshape(T, N_GROUP, gs), 2)
            group_scores = top2.sum(-1)
            _, gidx = jax.lax.top_k(group_scores, TOPK_GROUP)
            gmask = jax.nn.one_hot(gidx, N_GROUP, dtype=jnp.float32).sum(1)
            smask = jnp.repeat(gmask, gs, axis=1) > 0.5
            masked = jnp.where(smask, scores, 0.0)
            topk_idx = jax.lax.top_k(masked, TOP_K)[1]
            topk_w = jnp.take_along_axis(scores, topk_idx, axis=1)
            topk_w = topk_w / (topk_w.sum(-1, keepdims=True) + 1e-20)
            topk_w = topk_w * ROUTED_SCALING
            combine = jnp.zeros((T, E), jnp.float32).at[jnp.arange(T)[:, None], topk_idx].add(topk_w)
            return combine
        B, S, H = hidden_states.shape
        x = hidden_states.reshape(-1, H)
        combine = _route(x.astype(jnp.float32), gate_weight)
        up = jnp.einsum('th,ehi->eti', x, expert_up)
        down = jnp.einsum('eti,eih->eth', jax.nn.silu(up), expert_down)
        moe_out = jnp.einsum('te,eth->th', combine, down)
        shared = jax.nn.silu(x @ shared_up) @ shared_down
        return (moe_out + shared).reshape(B, S, H)
    h = _L0_tok_ref(x, L0_tok_W, L0_tok_b)
    h = jnp.concatenate([jnp.broadcast_to(cls_tok, (h.shape[0], 1, h.shape[2])), h], axis=1)
    h = h + _L0_attn_ref(_layernorm(h, axis=-1), L0_attn_Wq, L0_attn_bq, L0_attn_Wk, L0_attn_bk, L0_attn_Wv, L0_attn_bv, L0_attn_Wp, L0_attn_bp)
    h = h + _L0_ffn_ref(_layernorm(h, axis=-1), L0_ffn_gate_weight, L0_ffn_expert_up, L0_ffn_expert_down, L0_ffn_shared_up, L0_ffn_shared_down)
    return h

_drawn_inputs = setup_inputs


def setup_inputs(seed=0):
    import zlib

    import numpy as np

    out = dict(_drawn_inputs(seed))
    spreads = {}
    factors = {'cls_tok': 4.668,
     'L0_tok_b': 4.941,
     'L0_attn_Wq': 8.0,
     'L0_attn_bq': 8.0,
     'L0_attn_Wk': 8.0,
     'L0_attn_bk': 64.0,
     'L0_attn_Wv': 4.09,
     'L0_attn_bv': 6.819,
     'L0_attn_Wp': 3.664,
     'L0_attn_bp': 3.583}
    for name, (base, spread) in spreads.items():
        noise = np.random.default_rng([zlib.crc32(name.encode()), seed]).standard_normal(out[name].shape)
        drawn = base * np.exp(spread * noise) if base else spread * noise
        out[name] = jnp.asarray(drawn.astype(out[name].dtype))
    for name, factor in factors.items():
        out[name] = (out[name] * factor).astype(out[name].dtype)
    return out
```

```python
from contextlib import ExitStack

import numpy as np

import concourse.bass as bass
from concourse import mybir

F32 = mybir.dt.float32
F32R = mybir.dt.float32r
ACT = mybir.ActivationFunctionType
ALU = mybir.AluOpType
AX = mybir.AxisListType


def vit_block(nc, x, cls_tok, tok_W, tok_b, Wq, bq, Wk, bk, Wv, bv, Wp, bp,
              gate_W, expert_up, expert_down, shared_up, shared_down, out):
    B, CH, IMH, IMW = x.shape
    P = 16
    D = tok_W.shape[1]
    NH, NW = IMH // P, IMW // P
    T = NH * NW + 1
    E, _, I = expert_up.shape
    IS = shared_up.shape[1]
    HEADS, TOP_K, N_GROUP = 16, 4, 4
    DH = D // HEADS
    GS = E // N_GROUP
    DT = D // 128
    KT = CH * P * P // 128
    TT = 2 * T
    NTILE = B // 2
    NC = 4
    IC = B // NC
    TC = NTILE // NC
    N = IC * T
    HALF = B // 2
    RH = HALF * NH
    HT = NTILE // 2
    NPW = NW // 2
    NA = NPW * RH
    NSH = IS // I
    NU = E + NSH
    UG = 4
    NG = NU // UG
    PPM = 4
    VC = DH + 1
    EPS = 1e-5
    SCALE = float(DH) ** -0.5
    ROUTED = 2.5

    out_rows = out.rearrange("b t d -> (b t) d").rearrange("(c j p) d -> c p j d", c=NC, p=TT)

    ctx = ExitStack()
    tctx = ExitStack()
    with ctx:
        def sb(name, shape, dt=F32, where=ctx):
            return where.enter_context(nc.sbuf_tensor(name, shape, dt))

        def sem(name):
            return ctx.enter_context(nc.semaphore(name))

        ident = sb("ident", [128, 128])
        parity = sb("parity", [128, 2])
        parity_parts = sb("parity_parts", [128, 2, PPM])
        image_of = sb("image_of", [TT, 2])
        pick_r = sb("pick_r", [2 * E, E, 128], F32R)
        minus_half = sb("minus_half", [TT, HT])
        up_h = sb("up_h", [128, NU, DT, I], F32R)
        up_l = sb("up_l", [128, NU, DT, I], F32R)
        dn_h = sb("dn_h", [128, NU, D], F32R)
        dn_l = sb("dn_l", [128, NU, D], F32R)
        signT = sb("signT", [128, 4, DT, D], F32R)
        alpha = sb("alpha", [128, 4, DT])
        bias4 = sb("bias4", [128, 4, DT])
        q_scale = sb("q_scale", [128, DT, 2])
        q_bias = sb("q_bias", [128, DT, 2])
        tokb = sb("tokb", [128, DT])
        clsT = sb("clsT", [128, DT])
        gate_h = sb("gate_h", [128, DT, E], F32R)
        gate_l = sb("gate_l", [128, DT, E], F32R)
        h_tok = sb("h_tok", [TT, NTILE, D])
        xnT_h = sb("xnT_h", [128, DT, NTILE * TT], F32R)
        xnT_l = sb("xnT_l", [128, DT, NTILE * TT], F32R)

        XS = 2
        xs = sb("xs", [RH, XS, P // 2, IMW], where=tctx)
        xp = sb("xp", [RH, 2, NW, P // 2 * P], where=tctx)
        tokw = sb("tokw", [128, KT, D], where=tctx)
        tokw_h = sb("tokw_h", [128, KT, D], F32R, where=tctx)
        tokw_l = sb("tokw_l", [128, KT, D], F32R, where=tctx)
        hT = sb("hT", [128, DT, HALF, T], where=tctx)
        RAW = 3
        raw = sb("raw", [128, RAW, UG * DT * I], where=tctx)
        gate_w = sb("gate_w", [E, D], where=tctx)
        stats = sb("stats", [TT, HT, 6], where=tctx)
        mv = sb("mv", [TT, HT, 2], where=tctx)
        var_eps = sb("var_eps", [TT, HT], where=tctx)
        rstd = sb("rstd", [TT, HT], where=tctx)
        pick0 = sb("pick0", [2 * E, E, 128], where=tctx)
        with ExitStack() as early:
            wraw = sb("wraw", [128, 4, DT, D], where=early)
            wsign = sb("wsign", [128, 4, DT, D], where=early)
        PS = 2
        pt_h = sb("pt_h", [128, PS, 2, NA], F32R, where=tctx)
        pt_l = sb("pt_l", [128, PS, 2, NA], F32R, where=tctx)
        xn = sb("xn", [TT, HT, D], where=tctx)
        tctx.close()

        qblk = sb("qblk", [128, DT, IC, 2, T])
        kT = sb("kT", [128, DT, N])
        vT = sb("vT", [128, DT, N])
        vx = sb("vx", [TT, TC, HEADS, 2, VC])
        probs = sb("probs", [TT, 2, PPM, DT, 2, T])
        smax = sb("smax", [TT, 2, PPM * DT * 2])
        probsT = sb("probsT", [TT, 2, DT, PPM, TT])
        yrec = sb("yrec", [T, 2, DT, 2 * PPM, 2])
        y = sb("y", [T, TC, 2, D])
        yT_h = sb("yT_h", [128, DT, N], F32R)
        yT_l = sb("yT_l", [128, DT, N], F32R)
        attnT = sb("attnT", [128, DT, N])
        h2 = sb("h2", [TT, TC, D])
        stats2 = sb("stats2", [TT, TC, 6])
        mv2 = sb("mv2", [TT, TC, 2])
        var_eps2 = sb("var_eps2", [TT, TC])
        rstd2 = sb("rstd2", [TT, TC])
        xn2 = sb("xn2", [TT, TC, D])
        x2T_h = sb("x2T_h", [128, DT, N], F32R)
        x2T_l = sb("x2T_l", [128, DT, N], F32R)
        en = sb("en", [TT, TC, E])
        score = sb("score", [TT, TC, E])
        gsum6 = sb("gsum6", [TT, TC * N_GROUP, 6])
        gsum = sb("gsum", [TT, TC, N_GROUP])
        g_gt = sb("g_gt", [TT, TC, N_GROUP, N_GROUP])
        g_ge = sb("g_ge", [TT, TC, N_GROUP, N_GROUP])
        g_rank = sb("g_rank", [TT, TC, N_GROUP])
        g_in = sb("g_in", [TT, TC, N_GROUP])
        lower = sb("lower", [TT, N_GROUP, N_GROUP])
        masked = sb("masked", [TT, TC, E])
        top8 = sb("top8", [TT, TC, 8])
        above = sb("above", [TT, TC, E])
        n_above = sb("n_above", [TT, TC])
        PAD = 8
        run = [sb(f"run{i}", [TT, TC, PAD + E]) for i in range(2)]
        equal = sb("equal", [TT, TC, E])
        taken = sb("taken", [TT, TC, E])
        wsum = sb("wsum", [TT, TC])
        wrec = sb("wrec", [TT, TC])
        comb = sb("comb", [TT, TC, E])
        comb_r = sb("comb_r", [TT, TC, E], F32R)
        comb2 = sb("comb2", [TT, TC, 2, E])
        combT = sb("combT", [2 * E, N], F32R)
        th = sb("th", [128, 2, N])
        g1 = sb("g1", [128, 2, N])
        g2 = sb("g2", [128, 2, N])
        g_h = sb("g_h", [128, 2, N], F32R)
        g_l = sb("g_l", [128, 2, N], F32R)
        ffnT = sb("ffnT", [128, DT, N])
        res = xn2

        ps = ctx.enter_context(nc.psum_tensor("ps", [128, 8, 512], F32))

        ld_x = [sem(f"ld_x{i}") for i in range(2 * KT)]
        grouped = sem("grouped")
        ld_tokw, ld_attnw, ld_small, ld_gate = sem("ld_tokw"), sem("ld_attnw"), sem("ld_small"), sem("ld_gate")
        ld_unit = [sem(f"ld_unit{i}") for i in range(2 * NG)]
        pool_const = sem("pool_const")
        signs_done, alpha_done, pick_done = sem("signs_done"), sem("alpha_done"), sem("pick_done")
        signT_ps, signT_done = sem("signT_ps"), sem("signT_done")
        gateT_ps, gateT_h_done, gateT_done = sem("gateT_ps"), sem("gateT_h_done"), sem("gateT_done")
        tokw_h_done, tokw_done = sem("tokw_h_done"), sem("tokw_done")
        unit_h, unit_l = sem("unit_h"), sem("unit_l")
        patch_ps, patch_h, patch_l, patch_used = sem("patch_ps"), sem("patch_h"), sem("patch_l"), sem("patch_used")
        cls_done, emb_sb = sem("cls_done"), sem("emb_sb")
        tok_ps, tok_sb, aggr_done = sem("tok_ps"), sem("tok_sb"), sem("aggr_done")
        var_done, rstd_done, xn_done = sem("var_done"), sem("rstd_done"), sem("xn_done")
        xnT_ps, xnTh_done, xnTl_done = sem("xnT_ps"), sem("xnTh_done"), sem("xnTl_done")
        stats_done = sem("stats_done")
        qkv_ps, q_sb, kv_sb = sem("qkv_ps"), sem("q_sb"), sem("kv_sb")
        v_ps, vx_done = sem("v_ps"), sem("vx_done")
        s_ps, s_taken, p_done, max_done = sem("s_ps"), sem("s_taken"), sem("p_done"), sem("max_done")
        pT_ps, pT_sb = sem("pT_ps"), sem("pT_sb")
        y_ps, yrec_done, y_sb = sem("y_ps"), sem("yrec_done"), sem("y_sb")
        yT_ps, yTh_done, yTl_done = sem("yT_ps"), sem("yTh_done"), sem("yTl_done")
        proj_ps, proj_sb = sem("proj_ps"), sem("proj_sb")
        h2_ps, h2_done, stats2_done, aggr2_done = sem("h2_ps"), sem("h2_done"), sem("stats2_done"), sem("aggr2_done")
        var2_done, rstd2_done, xn2_done = sem("var2_done"), sem("rstd2_done"), sem("xn2_done")
        x2T_ps, x2Th_done, x2Tl_done = sem("x2T_ps"), sem("x2Th_done"), sem("x2Tl_done")
        logit_ps, en_done, route_step, comb_done = sem("logit_ps"), sem("en_done"), sem("route_step"), sem("comb_done")
        combT_ps, combT_sb = sem("combT_ps"), sem("combT_sb")
        u_ps, tanh_done, g1_done, w_ps, g2_done = sem("u_ps"), sem("tanh_done"), sem("g1_done"), sem("w_ps"), sem("g2_done")
        gh_done, gl_done, dn_used = sem("gh_done"), sem("gl_done"), sem("dn_used")
        ffn_sb, fT_ps, res_done, stored = sem("ffn_sb"), sem("fT_ps"), sem("res_done"), sem("stored")

        NTURN = 4 * DT

        def wait_gate(eng, c, u):
            if u < NSH:
                eng.wait_ge(g2_done, NU * c + u + 1)
            else:
                eng.wait_ge(g1_done, E * c + u - NSH + 1)

        registers = {}

        def wait_before(eng, once, least, semaphore, value):
            if eng not in registers:
                registers[eng] = eng.alloc_register(f"awaited{len(registers)}")
            eng.reg_mov(registers[eng], value)
            value = eng.snap(registers[eng])
            eng.wait_ge(once, least)
            eng.wait_ge(semaphore, value)

        block = ctx.enter_context(nc.Block())

        @block.sync
        def _(sp):
            xr = x.rearrange("b c (nh half py) w -> b c nh half (py w)", half=2, nh=NH)

            def load_x(n):
                g, k = divmod(n, KT)
                if n >= XS:
                    sp.wait_ge(grouped, n - XS + 1)
                src = xr[g * HALF:(g + 1) * HALF, k // 2, :, k % 2].rearrange("b r n -> b r n")
                sp.dma_start(xs[:, n % XS].rearrange("p y w -> p (y w)"), src).then_inc(ld_x[n], 16)

            load_x(0)
            sp.dma_start(tokw[:], tok_W.rearrange("(k p) d -> p k d", p=128)).then_inc(ld_tokw, 16)
            for n in range(1, XS):
                load_x(n)

            def load_unit(n):
                g, is_down = divmod(n, 2)
                if n >= RAW:
                    sp.wait_ge(unit_l, n - RAW + 1)
                slot = raw[:, n % RAW, :]
                if is_down:
                    dst = slot.rearrange("p (u d) -> p u d", u=UG)
                    src = (shared_down.rearrange("(u i) d -> i u d", i=I) if g == 0
                           else expert_down[(g - 1) * UG:g * UG].rearrange("u i d -> i u d"))
                    sp.dma_start(dst, src).then_inc(ld_unit[n], 16)
                elif g == 0:
                    for k in range(DT):
                        dst = slot.rearrange("p (u k i) -> p u k i", u=UG, k=DT)[:, :, k]
                        src = shared_up[k * 128:(k + 1) * 128].rearrange("p (u i) -> p u i", i=I)
                        sp.dma_start(dst, src).then_inc(ld_unit[n], 16)
                else:
                    dst = slot.rearrange("p (u i) -> p u i", u=UG * DT)
                    src = expert_up[(g - 1) * UG:g * UG].rearrange("u (k p) i -> p (u k) i", p=128)
                    sp.dma_start(dst, src).then_inc(ld_unit[n], 16)

            for n in range(XS, KT + XS):
                load_x(n)
            for n in range(NG):
                load_unit(n)
            for n in range(KT + XS, 2 * KT):
                load_x(n)
            for n in range(NG, 2 * NG):
                load_unit(n)
            def chunk(c):
                sp.wait_ge(res_done, TC * c + TC)
                sp.dma_start(out_rows[bass.ds(c, 1)].rearrange("a p j d -> p (a j) d"), res[:]).then_inc(stored, 16)

            chunk(0)
            with sp.Fori(1, NC) as c:
                chunk(c)
            sp.wait_ge(stored, 16 * NC)

        @block.gpsimd
        def _(pool):
            steps = [0]

            def const(ins):
                ins.then_inc(pool_const, 1)
                steps[0] += 1
                pool.wait_ge(pool_const, steps[0])

            const(pool.memset(ident[:], 0.0))
            const(pool.affine_select(out=ident[:], in_=ident[:], compare_op=ALU.not_equal, fill=1.0, base=0,
                                     pattern=[[-1, 128]], channel_multiplier=1))
            const(pool.memset(parity_parts[:], 1.0))
            const(pool.affine_select(out=parity_parts[:], in_=parity_parts[:], compare_op=ALU.is_ge, fill=0.0,
                                     base=0, pattern=[[-DH, 2], [-2 * DH, PPM]], channel_multiplier=1))
            const(pool.affine_select(out=parity_parts[:], in_=parity_parts[:], compare_op=ALU.is_ge, fill=0.0,
                                     base=DH - 1, pattern=[[DH, 2], [2 * DH, PPM]], channel_multiplier=-1))
            const(pool.memset(image_of[:], 1.0))
            const(pool.affine_select(out=image_of[:], in_=image_of[:], compare_op=ALU.is_ge, fill=0.0,
                                     base=0, pattern=[[-T, 2]], channel_multiplier=1))
            const(pool.affine_select(out=image_of[:], in_=image_of[:], compare_op=ALU.is_ge, fill=0.0,
                                     base=T - 1, pattern=[[T, 2]], channel_multiplier=-1))
            const(pool.memset(minus_half[:], -0.5))
            const(pool.memset(pick0[:], 0.0))
            for part in range(2):
                const(pool.affine_select(out=pick0[:], in_=pick0[:], compare_op=ALU.not_equal, fill=1.0,
                                         base=-E * part, pattern=[[-1, E], [0, 128]], channel_multiplier=1))

            for g in range(2):
                pool.wait_ge(aggr_done, HT * (g + 1))
                pool.tensor_scalar(var_eps[:], mv[:, :, 1], EPS, None, ALU.add).then_inc(var_done, 1)
                pool.wait_ge(var_done, g + 1)
                if g:
                    pool.wait_ge(xn_done, HT * g)
                pool.tensor_tensor(rstd[:], var_eps[:], minus_half[:], ALU.pow).then_inc(rstd_done, 1)

            def chunk(c):
                wait_before(pool, rstd_done, 2, aggr2_done, TC * c + TC)
                pool.tensor_scalar(var_eps2[:], mv2[:, :, 1], EPS, None, ALU.add).then_inc(var2_done, 1)
                pool.wait_ge(var2_done, c + 1)
                pool.tensor_tensor(rstd2[:], var_eps2[:], minus_half[:, 0:TC], ALU.pow).then_inc(rstd2_done, 1)

            chunk(0)
            with pool.Fori(1, NC) as c:
                chunk(c)

        @block.scalar
        def _(act):
            with nc.allow_non_contiguous_dma(reason="biases, a value per partition"):
                act.dma_start(tokb[:], tok_b.rearrange("(k p) -> p k", p=128)).then_inc(ld_small, 16)
                act.dma_start(clsT[:], cls_tok.rearrange("a b (k p) -> p (a b k)", p=128)).then_inc(ld_small, 16)
                for m, b in enumerate((bq, bk, bv, bp)):
                    act.dma_start(bias4[:, m], b.rearrange("(k p) -> p k", p=128)).then_inc(ld_small, 16)
            for m, w in enumerate((Wq, Wk, Wv, Wp)):
                act.dma_start(wraw[:, m], w.rearrange("(k p) c -> p k c", p=128)).then_inc(ld_attnw, 16)
            act.dma_start(gate_w[:], gate_W).then_inc(ld_gate, 16)

            act.wait_ge(ld_tokw, 16)
            act.activation(tokw_h[:], tokw[:], ACT.Copy).then_inc(tokw_h_done, 1)

            def split_patches(n):
                act.wait_ge(patch_ps, n + 1)
                if n == 0:
                    act.wait_ge(alpha_done, 1)
                if n >= PS:
                    act.wait_ge(patch_used, n - PS + 1)
                    act.wait_ge(patch_l, n - PS + 1)
                src = ps[:, 4 + 2 * (n % 2):6 + 2 * (n % 2), 0:NA]
                act.activation(pt_h[:, n % PS], src, ACT.Copy).then_inc(patch_h, 1)

            def signs():
                act.wait_ge(ld_attnw, 64)
                act.activation(wsign[:], wraw[:], ACT.Sign).then_inc(signs_done, 1)
                for n in range(NTURN):
                    act.wait_ge(signT_ps, n + 1)
                    m, ot = divmod(n, DT)
                    act.activation(signT[:, m, :, ot * 128:(ot + 1) * 128],
                                   ps[:, n % 4, 0:DT * 128].rearrange("p (k o) -> p k o", k=DT),
                                   ACT.Copy).then_inc(signT_done, 1)
                act.wait_ge(gateT_ps, 1)
                act.activation(gate_h[:], ps[:, 0, 0:DT * E].rearrange("p (k e) -> p k e", k=DT),
                               ACT.Copy).then_inc(gateT_h_done, 1)

            def unit_parts(n):
                g, is_down = divmod(n, 2)
                act.wait_ge(ld_unit[n], 32 if n == 0 else 16)
                dst = dn_h[:, g * UG:(g + 1) * UG] if is_down else up_h[:, g * UG:(g + 1) * UG]
                act.activation(dst.rearrange("p u d -> p (u d)") if is_down else dst.rearrange("p u k i -> p (u k i)"),
                               raw[:, n % RAW], ACT.Copy,
                               scale=0.5 if n == 1 else 1.0).then_inc(unit_h, 1)

            signs()
            for g in range(2):
                for k in range(KT):
                    split_patches(g * KT + k)
                act.wait_ge(patch_used, KT * (g + 1))
                act.wait_ge(ld_small, 96)
                if g:
                    act.wait_ge(tok_ps, HT * g)
                for dt in range(DT):
                    for w in range(2):
                        dst = hT[:, dt, :, 1:T].rearrange("p b (r w) -> p w b r", w=NW)[:, w * NPW:(w + 1) * NPW]
                        src = ps[:, 2 * dt + w, 0:NA].rearrange("p (w b r) -> p w b r", w=NPW, r=NH)
                        for i in range(NPW):
                            act.activation(dst[:, i], src[:, i], ACT.Identity,
                                           bias=tokb[:, dt:dt + 1]).then_inc(emb_sb, 1)
                for j in range(HT):
                    act.wait_ge(tok_ps, g * HT + j + 1)
                    act.activation(h_tok[:, g * HT + j], ps[0:TT, j % 4, 0:D], ACT.Copy).then_inc(tok_sb, 1)
                for n in range(NG * g, NG * (g + 1)):
                    unit_parts(n)
                for j in range(HT):
                    J = g * HT + j
                    act.wait_ge(xnT_ps, J + 1)
                    act.activation(xnT_h[:, :, J * TT:(J + 1) * TT],
                                   ps[:, j % 4, 0:DT * TT].rearrange("p (k t) -> p k t", k=DT),
                                   ACT.Copy).then_inc(xnTh_done, 1)

            def chunk(c):
                for mt in range(DT):
                    act.wait_ge(qkv_ps, 3 * DT * c + mt + 1)
                    if mt == 0:
                        act.wait_ge(alpha_done, 7)
                        act.wait_ge(s_ps, TC * c)
                    for a in range(2):
                        act.activation(qblk[:, mt, :, a, :],
                                       ps[:, mt, 0:N].rearrange("p (i t) -> p i t", t=T), ACT.Identity,
                                       scale=q_scale[:, mt, a:a + 1], bias=q_bias[:, mt, a:a + 1]).then_inc(q_sb, 1)
                for j in range(TC):
                    act.wait_ge(v_ps, TC * c + j + 1)
                    if j == 0:
                        act.wait_ge(route_step, 2 * TC)
                        act.wait_ge(y_ps, TC * c)
                    for i in range(2):
                        act.activation(vx[:, j, :, i, 0:DH],
                                       ps[0:TT, 6 + j % 2, 0:D].rearrange("p (h d) -> p h d", d=DH), ACT.Copy,
                                       scale=image_of[:, i:i + 1]).then_inc(vx_done, 1)
                for j in range(TC + 1):
                    if j < TC:
                        act.wait_ge(s_taken, TC * c + j + 1)
                        p = probs[:, j % 2].rearrange("p r m i s -> p (r m i s)")
                        act.activation(p, p, ACT.Exp).then_inc(p_done, 1)
                    if j >= 1:
                        act.wait_ge(pT_ps, TC * c + j)
                        if j - 1 < 2:
                            act.wait_ge(y_ps, TC * c + j - 1)
                        else:
                            act.wait_ge(y_ps, TC * c + j - 2)
                        act.activation(probsT[:, (j - 1) % 2].rearrange("p m r t -> p m (r t)"),
                                       ps[0:TT, 4:6, 0:PPM * TT], ACT.Copy).then_inc(pT_sb, 1)
                for j in range(TC):
                    act.wait_ge(yT_ps, TC * c + j + 1)
                    act.activation(yT_h[:, :, j * TT:(j + 1) * TT],
                                   ps[:, j, 0:DT * TT].rearrange("p (k t) -> p k t", k=DT),
                                   ACT.Copy).then_inc(yTh_done, 1)
                for ot in range(DT):
                    act.wait_ge(proj_ps, DT * c + ot + 1)
                    act.activation(attnT[:, ot], ps[:, 4 + ot, 0:N], ACT.Identity, scale=alpha[:, 3, ot:ot + 1],
                                   bias=bias4[:, 3, ot:ot + 1]).then_inc(proj_sb, 1)
                for j in range(TC):
                    act.wait_ge(x2T_ps, TC * c + j + 1)
                    act.activation(x2T_h[:, :, j * TT:(j + 1) * TT],
                                   ps[:, j, 0:DT * TT].rearrange("p (k t) -> p k t", k=DT),
                                   ACT.Copy).then_inc(x2Th_done, 1)
                act.wait_ge(logit_ps, c + 1)
                act.activation(en[:], ps[0:TT, 4, 0:TC * E].rearrange("p (j e) -> p j e", e=E), ACT.Exp,
                               scale=-1.0).then_inc(en_done, 1)

                def high_part(u):
                    act.wait_ge(g2_done, NU * c + u + 1)
                    act.wait_ge(dn_used, NU * c + max(u - 1, 0))
                    act.activation(g_h[:, u % 2], g2[:, u % 2], ACT.Copy).then_inc(gh_done, 1)

                for u in range(NU):
                    act.wait_ge(u_ps, NU * c + u + 1)
                    if u >= 2:
                        wait_gate(act, c, u - 2)
                    act.activation(th[:, u % 2], ps[:, 2 + u % 2, 0:N], ACT.Tanh, scale=0.5).then_inc(tanh_done, 1)
                    if u >= 1:
                        high_part(u - 1)
                high_part(NU - 1)
                act.wait_ge(dn_used, NU * c + NU)
                act.activation(ffnT[:], ps[:, 0:DT, 0:N], ACT.Copy).then_inc(ffn_sb, 1)

            chunk(0)
            with act.Fori(1, NC) as c:
                chunk(c)

        @block.vector
        def _(dve):
            dve.wait_ge(ld_attnw, 64)
            dve.tensor_reduce(alpha[:], wraw[:], AX.X, ALU.add, apply_absolute_value=True).then_inc(alpha_done, 1)
            dve.wait_ge(alpha_done, 1)
            dve.tensor_scalar(alpha[:], alpha[:], 1.0 / D, None, ALU.mult).then_inc(alpha_done, 1)
            dve.wait_ge(ld_tokw, 16)
            dve.wait_ge(tokw_h_done, 1)
            dve.tensor_tensor(tokw_l[:], tokw[:], tokw_h[:].bitcast(F32), ALU.subtract).then_inc(tokw_done, 1)
            dve.wait_ge(pool_const, 12)
            dve.tensor_reduce(parity[:], parity_parts[:], AX.X, ALU.add).then_inc(alpha_done, 1)
            dve.tensor_copy(pick_r[:], pick0[:]).then_inc(pick_done, 1)
            dve.wait_ge(alpha_done, 3)
            dve.wait_ge(ld_small, 96)
            for a in range(2):
                mask = parity[:, a:a + 1]
                dve.tensor_scalar(q_scale[:, :, a], alpha[:, 0], mask, SCALE, ALU.mult, ALU.mult).then_inc(alpha_done, 1)
                dve.tensor_scalar(q_bias[:, :, a], bias4[:, 0], mask, SCALE, ALU.mult, ALU.mult).then_inc(alpha_done, 1)
            dve.wait_ge(gateT_h_done, 1)
            dve.tensor_tensor(gate_l[:], ps[:, 0, 0:DT * E].rearrange("p (k e) -> p k e", k=DT),
                              gate_h[:].bitcast(F32), ALU.subtract).then_inc(gateT_done, 1)

            def unit_low(n):
                g, is_down = divmod(n, 2)
                dve.wait_ge(unit_h, n + 1)
                hi, lo = (dn_h, dn_l) if is_down else (up_h, up_l)
                flat = "p u d -> p (u d)" if is_down else "p u k i -> p (u k i)"
                hi = hi[:, g * UG:(g + 1) * UG].rearrange(flat)
                lo = lo[:, g * UG:(g + 1) * UG].rearrange(flat)
                dve.scalar_tensor_tensor(out=lo, in0=raw[:, n % RAW], scalar=0.5 if n == 1 else 1.0,
                                         in1=hi.bitcast(F32), op0=ALU.mult, op1=ALU.subtract).then_inc(unit_l, 1)

            def group_pixels(n):
                dve.wait_ge(ld_x[n], 16)
                if n >= 2:
                    dve.wait_ge(patch_ps, n - 1)
                dve.tensor_copy(xp[:, n % 2].rearrange("p w (y x) -> p w y x", x=P),
                                xs[:, n % XS].rearrange("p y (w x) -> p w y x", x=P)).then_inc(grouped, 1)

            group_pixels(0)
            for g in range(2):
                for k in range(KT):
                    n = g * KT + k
                    if n + 1 < 2 * KT:
                        group_pixels(n + 1)
                    dve.wait_ge(patch_h, n + 1)
                    if n >= PS:
                        dve.wait_ge(patch_used, n - PS + 1)
                    dve.tensor_tensor(pt_l[:, n % PS], ps[:, 4 + 2 * (n % 2):6 + 2 * (n % 2), 0:NA],
                                      pt_h[:, n % PS].bitcast(F32), ALU.subtract).then_inc(patch_l, 1)
                if g:
                    dve.wait_ge(tok_ps, HT * g)
                for dt in range(DT):
                    dve.tensor_copy(hT[:, dt, :, 0], clsT[:, dt:dt + 1].to_broadcast([128, HALF])).then_inc(cls_done, 1)
                for j in range(HT):
                    J = g * HT + j
                    dve.wait_ge(tok_sb, J + 1)
                    if g and j == 0:
                        dve.wait_ge(aggr_done, HT * g)
                    dve.bn_stats(stats[:, j], h_tok[:, J]).then_inc(stats_done, 1)
                if g:
                    dve.wait_ge(var_done, g)
                    dve.wait_ge(xn_done, HT * g)
                for j in range(HT):
                    dve.wait_ge(stats_done, g * HT + j + 1)
                    dve.bn_aggr(mv[:, j], stats[:, j]).then_inc(aggr_done, 1)
                dve.wait_ge(rstd_done, g + 1)
                dve.wait_ge(aggr_done, HT * (g + 1))
                for j in range(HT):
                    J = g * HT + j
                    if g:
                        dve.wait_ge(xnT_ps, HT * (g - 1) + j + 1)
                    dve.tensor_scalar(xn[:, j], h_tok[:, J], mv[:, j, 0:1], rstd[:, j:j + 1],
                                      ALU.subtract, ALU.mult).then_inc(xn_done, 1)
                for n in range(NG * g, NG * (g + 1)):
                    unit_low(n)
                for j in range(HT):
                    J = g * HT + j
                    dve.wait_ge(xnTh_done, J + 1)
                    dve.tensor_tensor(xnT_l[:, :, J * TT:(J + 1) * TT],
                                      ps[:, j % 4, 0:DT * TT].rearrange("p (k t) -> p k t", k=DT),
                                      xnT_h[:, :, J * TT:(J + 1) * TT].bitcast(F32),
                                      ALU.subtract).then_inc(xnTl_done, 1)

            dve.wait_ge(xnTl_done, NTILE)
            dve.wait_ge(unit_l, 2 * NG)
            dve.wait_ge(xnT_ps, NTILE)
            for i in range(2):
                for j in range(TC):
                    dve.tensor_copy(vx[:, j, :, i, DH], image_of[:, i:i + 1].to_broadcast([TT, HEADS])).then_inc(route_step, 1)
            for b in run:
                dve.memset(b[:, :, 0:PAD], 0.0).then_inc(route_step, 1)
            dve.memset(lower[:], 0.0).then_inc(route_step, 1)
            K0 = 2 * TC + 3
            dve.wait_ge(route_step, K0)
            for g in range(1, N_GROUP):
                dve.memset(lower[:, g, 0:g], 1.0).then_inc(route_step, 1)
            K0 += N_GROUP - 1
            dve.wait_ge(route_step, K0)

            STEPS = 28
            def chunk(c):
                for mt in range(DT):
                    for m, dst in ((1, kT), (2, vT)):
                        dve.wait_ge(qkv_ps, 3 * DT * c + m * DT + mt + 1)
                        if mt == 0:
                            dve.wait_ge(s_ps if m == 1 else v_ps, TC * c)
                        dve.tensor_scalar(dst[:, mt], ps[:, m * DT + mt, 0:N], alpha[:, m, mt:mt + 1],
                                          bias4[:, m, mt:mt + 1], ALU.mult, ALU.add).then_inc(kv_sb, 1)

                def take_scores(j):
                    S = ps[0:TT, 0:PPM, 0:DT * TT].rearrange("p r (m s) -> p r m s", s=T)
                    P4 = probs[:, j % 2].rearrange("p r m i s -> p r (m i) s")
                    dve.wait_ge(s_ps, TC * c + j + 1)
                    if j >= 2:
                        dve.wait_ge(s_taken, TC * c + j - 1)
                    else:
                        dve.wait_ge(s_taken, TC * c + j)
                    m = smax[:, j % 2]
                    dve.tensor_reduce(m.rearrange("p (r m) -> p r m", r=PPM), S, AX.X, ALU.max).then_inc(max_done, 1)
                    dve.wait_ge(max_done, TC * c + j + 1)
                    dve.wait_ge(pT_ps, TC * c + max(j - 1, 0))
                    for r in range(PPM):
                        ins = dve.tensor_tensor(P4[:, r], S[:, r],
                                                m[:, r * 2 * DT:(r + 1) * 2 * DT, None].to_broadcast([TT, 2 * DT, T]),
                                                ALU.subtract)
                    ins.then_inc(s_taken, 1)

                def take_y(j):
                    dve.wait_ge(y_ps, TC * c + j + 1)
                    Y = ps[0:T, 6:8, 0:2 * PPM * 2 * VC].rearrange("p m (h i v) -> p m h i v", i=2, v=VC)
                    if j >= 2:
                        dve.wait_ge(y_sb, DT * (TC * c + j - 1))
                    dve.reciprocal(yrec[:, j % 2], Y[:, :, :, :, DH]).then_inc(yrec_done, 1)
                    dve.wait_ge(yrec_done, TC * c + j + 1)
                    if j == 0:
                        dve.wait_ge(yT_ps, TC * c)
                    for mt in range(DT):
                        dst = y[:, j].rearrange("p i (m h d) -> p m h i d", m=DT, d=DH)[:, mt]
                        dve.tensor_tensor(dst, Y[:, mt, :, :, 0:DH],
                                          yrec[:, j % 2, mt, :, :, None].to_broadcast([T, 2 * PPM, 2, DH]),
                                          ALU.mult).then_inc(y_sb, 1)

                take_scores(0)
                for j in range(TC):
                    if j + 1 < TC:
                        take_scores(j + 1)
                    take_y(j)
                for j in range(TC):
                    dve.wait_ge(yTh_done, TC * c + j + 1)
                    dve.tensor_tensor(yT_l[:, :, j * TT:(j + 1) * TT],
                                      ps[:, j, 0:DT * TT].rearrange("p (k t) -> p k t", k=DT),
                                      yT_h[:, :, j * TT:(j + 1) * TT].bitcast(F32),
                                      ALU.subtract).then_inc(yTl_done, 1)
                for j in range(TC):
                    dve.wait_ge(h2_ps, TC * c + j + 1)
                    dve.tensor_tensor(h2[:, j], ps[0:TT, 6 + j % 2, 0:D],
                                      h_tok[:, bass.ds(TC * c + j, 1), :].rearrange("p a d -> p (a d)"),
                                      ALU.add).then_inc(h2_done, 1)
                for j in range(TC):
                    dve.wait_ge(h2_done, TC * c + j + 1)
                    dve.bn_stats(stats2[:, j], h2[:, j]).then_inc(stats2_done, 1)
                for j in range(TC):
                    wait_before(dve, aggr_done, NTILE, stats2_done, TC * c + j + 1)
                    dve.bn_aggr(mv2[:, j], stats2[:, j]).then_inc(aggr2_done, 1)
                dve.wait_ge(aggr2_done, TC * c + TC)
                dve.wait_ge(rstd2_done, c + 1)
                dve.wait_ge(stored, 16 * c)
                for j in range(TC):
                    dve.tensor_scalar(xn2[:, j], h2[:, j], mv2[:, j, 0:1], rstd2[:, j:j + 1],
                                      ALU.subtract, ALU.mult).then_inc(xn2_done, 1)
                for j in range(TC):
                    dve.wait_ge(x2Th_done, TC * c + j + 1)
                    dve.tensor_tensor(x2T_l[:, :, j * TT:(j + 1) * TT],
                                      ps[:, j, 0:DT * TT].rearrange("p (k t) -> p k t", k=DT),
                                      x2T_h[:, :, j * TT:(j + 1) * TT].bitcast(F32),
                                      ALU.subtract).then_inc(x2Tl_done, 1)

                n = [0]

                def link(ins, before_max=False):
                    ins.then_inc(route_step, 1)
                    n[0] += 1
                    if before_max:
                        wait_before(dve, aggr_done, NTILE, route_step, c * STEPS + (K0 + n[0]))
                    else:
                        dve.wait_ge(route_step, c * STEPS + (K0 + n[0]))

                dve.wait_ge(en_done, c + 1)
                link(dve.tensor_scalar(en[:], en[:], 1.0, None, ALU.add))
                link(dve.reciprocal(score[:], en[:]))
                sc4 = score[:].rearrange("p j (g s) -> p (j g) s", s=GS)
                at = 0
                for d in range(1, GS):
                    ins = dve.tensor_tensor(gsum6[:, :, at:at + GS - d], sc4[:, :, 0:GS - d], sc4[:, :, d:GS], ALU.add)
                    at += GS - d
                    link(ins)
                link(dve.tensor_reduce(gsum[:].rearrange("p j g -> p (j g)"), gsum6[:], AX.X, ALU.max))
                for j in range(TC):
                    rival = gsum[:, j, None, :].to_broadcast([TT, N_GROUP, N_GROUP])
                    own = gsum[:, j, :, None].to_broadcast([TT, N_GROUP, N_GROUP])
                    dve.tensor_tensor(g_gt[:, j], rival, own, ALU.is_gt)
                    ins = dve.tensor_tensor(g_ge[:, j], rival, own, ALU.is_equal)
                link(ins)
                for j in range(TC):
                    ins = dve.tensor_tensor(g_ge[:, j], g_ge[:, j], lower[:], ALU.mult)
                link(ins)
                link(dve.tensor_tensor(g_gt[:], g_gt[:], g_ge[:], ALU.add))
                link(dve.tensor_reduce(g_rank[:].rearrange("p j g -> p (j g)"),
                                       g_gt[:].rearrange("p j g r -> p (j g) r"), AX.X, ALU.add))
                link(dve.tensor_scalar(g_in[:], g_rank[:], 1.5, None, ALU.is_lt))
                link(dve.tensor_tensor(masked[:].rearrange("p j (g s) -> p (j g) s", s=GS), sc4,
                                       g_in[:].rearrange("p j g -> p (j g)")[:, :, None].to_broadcast([TT, TC * N_GROUP, GS]),
                                       ALU.mult), before_max=True)
                for j in range(TC):
                    ins = dve.max(top8[:, j], masked[:, j])
                link(ins)
                kth = top8[:, :, TOP_K - 1:TOP_K].to_broadcast([TT, TC, E])
                dve.tensor_tensor(above[:], masked[:], kth, ALU.is_gt)
                dve.tensor_tensor(equal[:], masked[:], kth, ALU.is_equal)
                link(dve.tensor_tensor(run[0][:, :, PAD:], masked[:], kth, ALU.is_equal))
                link(dve.tensor_reduce(n_above[:], above[:], AX.X, ALU.add))
                for s in range(4):
                    a, b = run[s % 2], run[1 - s % 2]
                    link(dve.tensor_tensor(b[:, :, PAD:], a[:, :, PAD:], a[:, :, PAD - (1 << s):PAD - (1 << s) + E], ALU.add))
                link(dve.tensor_tensor(run[1][:, :, PAD:], run[0][:, :, PAD:],
                                       n_above[:, :, None].to_broadcast([TT, TC, E]), ALU.add))
                link(dve.tensor_scalar(run[1][:, :, PAD:], run[1][:, :, PAD:], TOP_K + 0.5, None, ALU.is_lt))
                link(dve.tensor_tensor(taken[:], run[1][:, :, PAD:], equal[:], ALU.mult))
                link(dve.tensor_tensor(taken[:], taken[:], above[:], ALU.add))
                link(dve.tensor_tensor(taken[:], taken[:], score[:], ALU.mult))
                link(dve.tensor_reduce(wsum[:], taken[:], AX.X, ALU.add))
                link(dve.tensor_scalar(wsum[:], wsum[:], 1e-20, None, ALU.add))
                link(dve.reciprocal(wrec[:], wsum[:]))
                link(dve.scalar_tensor_tensor(out=comb[:], in0=taken[:], scalar=0.5 * ROUTED,
                                              in1=wrec[:, :, None].to_broadcast([TT, TC, E]), op0=ALU.mult, op1=ALU.mult))
                assert n[0] == STEPS, n[0]
                dve.tensor_copy(comb_r[:], comb[:]).then_inc(comb_done, 1)
                dve.wait_ge(comb_done, 3 * c + 1)
                dve.tensor_copy(comb2[:, :, 0], comb_r[:].bitcast(F32)).then_inc(comb_done, 1)
                dve.tensor_tensor(comb2[:, :, 1], comb[:], comb_r[:].bitcast(F32), ALU.subtract).then_inc(comb_done, 1)

                def low_part(u):
                    dve.wait_ge(gh_done, NU * c + u + 1)
                    dve.tensor_tensor(g_l[:, u % 2], g2[:, u % 2], g_h[:, u % 2].bitcast(F32),
                                      ALU.subtract).then_inc(gl_done, 1)

                for u in range(NU):
                    if u == NSH:
                        dve.wait_ge(combT_ps, c + 1)
                        dve.tensor_copy(combT[:], ps[0:2 * E, 5, 0:N]).then_inc(combT_sb, 1)
                    dve.wait_ge(tanh_done, NU * c + u + 1)
                    dve.wait_ge(gl_done, NU * c + max(u - 1, 0))
                    gate = g2 if u < NSH else g1
                    ins = dve.scalar_tensor_tensor(out=gate[:, u % 2], in0=th[:, u % 2], scalar=1.0,
                                                   in1=ps[:, 2 + u % 2, 0:N], op0=ALU.add, op1=ALU.mult)
                    if u < NSH:
                        ins.then_inc(g2_done, 1)
                    else:
                        ins.then_inc(g1_done, 1)
                        dve.wait_ge(g1_done, E * c + u - NSH + 1)
                        dve.wait_ge(w_ps, E * c + u - NSH + 1)
                        dve.tensor_tensor(g2[:, u % 2], g1[:, u % 2], ps[:, 4 + u % 2, 0:N], ALU.mult).then_inc(g2_done, 1)
                    if u >= 1:
                        low_part(u - 1)
                low_part(NU - 1)
                for j in range(TC):
                    dve.wait_ge(fT_ps, TC * c + j + 1)
                    dve.tensor_tensor(res[:, j], ps[0:TT, 6 + j % 2, 0:D], h2[:, j], ALU.add).then_inc(res_done, 1)

            chunk(0)
            with dve.Fori(1, NC) as c:
                chunk(c)

        @block.tensor
        def _(pe):
            pe.wait_ge(pool_const, 2)
            pe.wait_ge(signs_done, 1)
            for n in range(NTURN):
                m, ot = divmod(n, DT)
                if n >= 4:
                    pe.wait_ge(signT_done, n - 3)
                for kt in range(DT):
                    mm = pe.transpose(ps[:, n % 4, kt * 128:(kt + 1) * 128], wsign[:, m, ot, kt * 128:(kt + 1) * 128], ident[:])
                mm.then_inc(signT_ps, 1)
            pe.wait_ge(ld_gate, 16)
            pe.wait_ge(signT_done, NTURN)
            for kt in range(DT):
                mm = pe.transpose(ps[:, 0, kt * E:(kt + 1) * E], gate_w[:, kt * 128:(kt + 1) * 128], ident[0:E, 0:E])
            mm.then_inc(gateT_ps, 1)

            def turn_patches(n):
                g, k = divmod(n, KT)
                pe.wait_ge(grouped, n + 1)
                if n >= 2:
                    pe.wait_ge(patch_l, n - 1)
                for w in range(NW):
                    src = xp[:, n % 2, w]
                    mm = pe.transpose(ps[:, 4 + 2 * (n % 2) + w // NPW, (w % NPW) * RH:(w % NPW + 1) * RH], src,
                                      ident[0:RH, 0:RH])
                mm.then_inc(patch_ps, 1)

            def embed(n):
                g, k = divmod(n, KT)
                pe.wait_ge(tokw_done, 1)
                pe.wait_ge(patch_l, n + 1)
                if k == 0:
                    pe.wait_ge(gateT_done, 1)
                    if g:
                        pe.wait_ge(xnTl_done, HT * g)
                for dt in range(DT):
                    for w in range(2):
                        for i, (a, b) in enumerate(((tokw_h, pt_h), (tokw_h, pt_l), (tokw_l, pt_h))):
                            mm = pe.matmul(ps[:, 2 * dt + w, 0:NA], a[:, k, dt * 128:(dt + 1) * 128], b[:, n % PS, w],
                                           start=(k == 0 and i == 0), stop=(k == KT - 1 and i == 2))
                mm.then_inc(patch_used, 1)

            for g in range(2):
                if g == 0:
                    turn_patches(0)
                for k in range(KT):
                    n = g * KT + k
                    if n + 1 < 2 * KT:
                        turn_patches(n + 1)
                    embed(n)
                pe.wait_ge(emb_sb, 2 * DT * NPW * (g + 1))
                pe.wait_ge(cls_done, DT * (g + 1))
                for j in range(HT):
                    if j >= 4:
                        pe.wait_ge(tok_sb, g * HT + j - 3)
                    for dt in range(DT):
                        src = hT[:, dt].rearrange("p b t -> p (b t)")[:, j * TT:(j + 1) * TT]
                        mm = pe.transpose(ps[0:TT, j % 4, dt * 128:(dt + 1) * 128], src, ident[:])
                    mm.then_inc(tok_ps, 1)
                pe.wait_ge(tok_sb, HT * (g + 1))
                for j in range(HT):
                    pe.wait_ge(xn_done, g * HT + j + 1)
                    if j >= 4:
                        pe.wait_ge(xnTl_done, g * HT + j - 3)
                    for kt in range(DT):
                        mm = pe.transpose(ps[:, j % 4, kt * TT:(kt + 1) * TT], xn[:, j, kt * 128:(kt + 1) * 128],
                                          ident[0:TT, 0:TT])
                    mm.then_inc(xnT_ps, 1)

            pe.wait_ge(xnTl_done, NTILE)
            pe.wait_ge(unit_l, 2 * NG)
            def chunk(c):
                pe.wait_ge(res_done, TC * c)
                for m in range(3):
                    for mt in range(DT):
                        for kt in range(DT):
                            for i, b in enumerate((xnT_h, xnT_l)):
                                mm = pe.matmul(ps[:, m * DT + mt, 0:N], signT[:, m, kt, mt * 128:(mt + 1) * 128],
                                               b[:, kt, bass.ds(N * c, N)], start=(kt == 0 and i == 0),
                                               stop=(kt == DT - 1 and i == 1))
                        mm.then_inc(qkv_ps, 1)
                pe.wait_ge(kv_sb, 2 * DT * c + 2 * DT)
                for j in range(TC):
                    if j >= 2:
                        pe.wait_ge(vx_done, 2 * (TC * c + j - 1))
                    for mt in range(DT):
                        mm = pe.transpose(ps[0:TT, 6 + j % 2, mt * 128:(mt + 1) * 128], vT[:, mt, j * TT:(j + 1) * TT], ident[:])
                    mm.then_inc(v_ps, 1)

                def scores(j):
                    if j == 0:
                        pe.wait_ge(q_sb, 2 * DT * c + 2 * DT)
                    else:
                        pe.wait_ge(s_taken, TC * c + j)
                    for mt in range(DT):
                        for i in range(2):
                            for r in range(PPM):
                                rows = slice(32 * r, 32 * r + 32)
                                img = 2 * j + i
                                mm = pe.matmul(ps[0:TT, r, mt * TT + i * T:mt * TT + (i + 1) * T],
                                               qblk[rows, mt, img].rearrange("p a t -> p (a t)"),
                                               kT[rows, mt, img * T:(img + 1) * T], start=True, stop=True)
                    mm.then_inc(s_ps, 1)

                scores(0)
                for j in range(TC):
                    if j + 1 < TC:
                        scores(j + 1)
                    pe.wait_ge(p_done, TC * c + j + 1)
                    pe.wait_ge(pT_sb, TC * c + j)
                    for mt in range(DT):
                        for r in range(PPM):
                            mm = pe.transpose(ps[0:TT, 4 + mt, r * TT:(r + 1) * TT],
                                              probs[:, j % 2, r, mt].rearrange("p i s -> p (i s)"), ident[0:TT, 0:TT])
                    mm.then_inc(pT_ps, 1)
                    pe.wait_ge(pT_sb, TC * c + j + 1)
                    if j == 0:
                        pe.wait_ge(vx_done, 2 * TC * c + 2 * TC)
                    pe.wait_ge(y_sb, DT * (TC * c + j))
                    for mt in range(DT):
                        for r in range(PPM):
                            for a in range(2):
                                h = 2 * r + a
                                mm = pe.matmul(ps[0:T, 6 + mt, h * 2 * VC:(h + 1) * 2 * VC],
                                               probsT[:, j % 2, mt, r, a * T:(a + 1) * T],
                                               vx[:, j, mt * 2 * PPM + h].rearrange("p i v -> p (i v)"),
                                               start=True, stop=True)
                    mm.then_inc(y_ps, 1)
                for j in range(TC):
                    wait_before(pe, pool_const, 2, y_sb, DT * (TC * c + j + 1))
                    for mt in range(DT):
                        for i in range(2):
                            mm = pe.transpose(ps[:, j, mt * TT + i * T:mt * TT + (i + 1) * T],
                                              y[:, j, i, mt * 128:(mt + 1) * 128], ident[0:T, 0:T])
                    mm.then_inc(yT_ps, 1)
                pe.wait_ge(yTl_done, TC * c + TC)
                for ot in range(DT):
                    for kt in range(DT):
                        for i, b in enumerate((yT_h, yT_l)):
                            mm = pe.matmul(ps[:, 4 + ot, 0:N], signT[:, 3, kt, ot * 128:(ot + 1) * 128], b[:, kt],
                                           start=(kt == 0 and i == 0), stop=(kt == DT - 1 and i == 1))
                    mm.then_inc(proj_ps, 1)
                pe.wait_ge(proj_sb, DT * c + DT)
                for j in range(TC):
                    if j >= 2:
                        pe.wait_ge(h2_done, TC * c + j - 1)
                    for ot in range(DT):
                        mm = pe.transpose(ps[0:TT, 6 + j % 2, ot * 128:(ot + 1) * 128], attnT[:, ot, j * TT:(j + 1) * TT], ident[:])
                    mm.then_inc(h2_ps, 1)
                for j in range(TC):
                    pe.wait_ge(xn2_done, TC * c + j + 1)
                    for kt in range(DT):
                        mm = pe.transpose(ps[:, j, kt * TT:(kt + 1) * TT], xn2[:, j, kt * 128:(kt + 1) * 128], ident[0:TT, 0:TT])
                    mm.then_inc(x2T_ps, 1)
                pe.wait_ge(x2Tl_done, TC * c + TC)
                for j in range(TC):
                    cols = slice(j * TT, (j + 1) * TT)
                    for kt in range(DT):
                        for i, (a, b) in enumerate(((x2T_h, gate_h), (x2T_l, gate_h), (x2T_h, gate_l))):
                            mm = pe.matmul(ps[0:TT, 4, j * E:(j + 1) * E], a[:, kt, cols], b[:, kt],
                                           start=(kt == 0 and i == 0), stop=(kt == DT - 1 and i == 2))
                mm.then_inc(logit_ps, 1)

                def up(u):
                    if u >= 2:
                        wait_gate(pe, c, u - 2)
                    for kt in range(DT):
                        for i, (a, b) in enumerate(((up_h, x2T_h), (up_h, x2T_l), (up_l, x2T_h))):
                            mm = pe.matmul(ps[:, 2 + u % 2, 0:N], a[:, u, kt], b[:, kt],
                                           start=(kt == 0 and i == 0), stop=(kt == DT - 1 and i == 2))
                    mm.then_inc(u_ps, 1)

                def spread(e):
                    if e == 0:
                        pe.wait_ge(comb_done, 3 * c + 3)
                        for j in range(TC):
                            mm = pe.transpose(ps[0:2 * E, 5, j * TT:(j + 1) * TT],
                                              comb2[:, j].rearrange("p a e -> p (a e)"), ident[0:TT, 0:TT])
                        mm.then_inc(combT_ps, 1)
                        pe.wait_ge(combT_sb, c + 1)
                    if e >= 2:
                        pe.wait_ge(g2_done, NU * c + NSH + e - 1)
                    pe.matmul(ps[:, 4 + e % 2, 0:N], pick_r[:, e], combT[:], start=True, stop=True).then_inc(w_ps, 1)

                def down(u):
                    pe.wait_ge(gl_done, NU * c + u + 1)
                    for dt in range(DT):
                        w = slice(dt * 128, (dt + 1) * 128)
                        for i, (a, b) in enumerate(((dn_h, g_h), (dn_h, g_l), (dn_l, g_h))):
                            mm = pe.matmul(ps[:, dt, 0:N], a[:, u, w], b[:, u % 2],
                                           start=(u == 0 and i == 0), stop=(u == NU - 1 and i == 2))
                    mm.then_inc(dn_used, 1)

                up(0)
                for u in range(NU):
                    if u + 1 < NU:
                        up(u + 1)
                        if u + 1 >= NSH:
                            spread(u + 1 - NSH)
                    down(u)
                pe.wait_ge(ffn_sb, c + 1)
                for j in range(TC):
                    if j >= 2:
                        pe.wait_ge(res_done, TC * c + j - 1)
                    for dt in range(DT):
                        mm = pe.transpose(ps[0:TT, 6 + j % 2, dt * 128:(dt + 1) * 128], ffnT[:, dt, j * TT:(j + 1) * TT], ident[:])
                    mm.then_inc(fT_ps, 1)

            chunk(0)
            with pe.Fori(1, NC) as c:
                chunk(c)

_INS = ["x", "cls_tok", "L0_tok_W", "L0_tok_b", "L0_attn_Wq", "L0_attn_bq", "L0_attn_Wk", "L0_attn_bk",
        "L0_attn_Wv", "L0_attn_bv", "L0_attn_Wp", "L0_attn_bp", "L0_ffn_gate_weight", "L0_ffn_expert_up",
        "L0_ffn_expert_down", "L0_ffn_shared_up", "L0_ffn_shared_down"]


def kernel(**inputs):
    import concourse.bacc as bacc
    from concourse.bass_utils import run_bass_kernel_spmd

    nc = bacc.Bacc("TRN2", target_bir_lowering=False, num_devices=1)
    arrays, args = {}, []
    for name in _INS:
        a = np.ascontiguousarray(inputs[name])
        arrays[f"in_{name}"] = a
        args.append(nc.dram_tensor(f"in_{name}", a.shape, F32, kind="ExternalInput").ap())
    B, _, H, W = inputs["x"].shape
    D = inputs["L0_tok_W"].shape[1]
    shape = (B, (H // 16) * (W // 16) + 1, D)
    args.append(nc.dram_tensor("out_h", shape, F32, kind="ExternalOutput").ap())
    vit_block(nc, *args)
    r = run_bass_kernel_spmd(nc, [arrays], core_ids=[0])
    return r.results[0]["out_h"]
```

```python
from contextlib import ExitStack

import numpy as np

import concourse.bass as bass
from concourse import mybir

F32 = mybir.dt.float32
F32R = mybir.dt.float32r
ACT = mybir.ActivationFunctionType
ALU = mybir.AluOpType
AX = mybir.AxisListType


def vit_block(nc, x, cls_tok, tok_W, tok_b, Wq, bq, Wk, bk, Wv, bv, Wp, bp,
              gate_W, expert_up, expert_down, shared_up, shared_down, out):
    B, CH, IMH, IMW = x.shape
    P = 16
    D = tok_W.shape[1]
    NH, NW = IMH // P, IMW // P
    T = NH * NW + 1
    E, _, I = expert_up.shape
    IS = shared_up.shape[1]
    HEADS, TOP_K, N_GROUP = 16, 4, 4
    DH = D // HEADS
    GS = E // N_GROUP
    DT = D // 128
    KT = CH * P * P // 128
    TT = 2 * T
    NTILE = B // 2
    NC = 4
    IC = B // NC
    TC = NTILE // NC
    N = IC * T
    HALF = B // 2
    RH = HALF * NH
    HT = NTILE // 2
    NPW = NW // 2
    NA = NPW * RH
    NSH = IS // I
    NU = E + NSH
    UG = 4
    NG = NU // UG
    PPM = 4
    VC = DH + 1
    EPS = 1e-5
    SCALE = float(DH) ** -0.5
    ROUTED = 2.5

    out_rows = out.rearrange("b t d -> (b t) d").rearrange("(c j p) d -> c p j d", c=NC, p=TT)

    ctx = ExitStack()
    tctx = ExitStack()
    with ctx:
        def sb(name, shape, dt=F32, where=ctx):
            return where.enter_context(nc.sbuf_tensor(name, shape, dt))

        def sem(name):
            return ctx.enter_context(nc.semaphore(name))

        ident = sb("ident", [128, 128])
        parity = sb("parity", [128, 2])
        parity_parts = sb("parity_parts", [128, 2, PPM])
        image_of = sb("image_of", [TT, 2])
        pick_r = sb("pick_r", [2 * E, E, 128], F32R)
        minus_half = sb("minus_half", [TT, HT])
        up_h = sb("up_h", [128, NU, DT, I], F32R)
        up_l = sb("up_l", [128, NU, DT, I], F32R)
        dn_h = sb("dn_h", [128, NU, D], F32R)
        dn_l = sb("dn_l", [128, NU, D], F32R)
        signT = sb("signT", [128, 4, DT, D], F32R)
        alpha = sb("alpha", [128, 4, DT])
        bias4 = sb("bias4", [128, 4, DT])
        q_scale = sb("q_scale", [128, DT, 2])
        q_bias = sb("q_bias", [128, DT, 2])
        tokb = sb("tokb", [128, DT])
        clsT = sb("clsT", [128, DT])
        gate_h = sb("gate_h", [128, DT, E], F32R)
        gate_l = sb("gate_l", [128, DT, E], F32R)
        h_tok = sb("h_tok", [TT, NTILE, D])
        xnT_h = sb("xnT_h", [128, DT, NTILE * TT], F32R)
        xnT_l = sb("xnT_l", [128, DT, NTILE * TT], F32R)

        XS = 2
        xs = sb("xs", [RH, XS, P // 2, IMW], where=tctx)
        xp = sb("xp", [RH, 2, NW, P // 2 * P], where=tctx)
        tokw = sb("tokw", [128, KT, D], where=tctx)
        tokw_h = sb("tokw_h", [128, KT, D], F32R, where=tctx)
        tokw_l = sb("tokw_l", [128, KT, D], F32R, where=tctx)
        hT = sb("hT", [128, DT, HALF, T], where=tctx)
        RAW = 3
        raw = sb("raw", [128, RAW, UG * DT * I], where=tctx)
        gate_w = sb("gate_w", [E, D], where=tctx)
        stats = sb("stats", [TT, HT, 6], where=tctx)
        mv = sb("mv", [TT, HT, 2], where=tctx)
        var_eps = sb("var_eps", [TT, HT], where=tctx)
        rstd = sb("rstd", [TT, HT], where=tctx)
        pick0 = sb("pick0", [2 * E, E, 128], where=tctx)
        with ExitStack() as early:
            wraw = sb("wraw", [128, 4, DT, D], where=early)
            wsign = sb("wsign", [128, 4, DT, D], where=early)
        PS = 2
        pt_h = sb("pt_h", [128, PS, 2, NA], F32R, where=tctx)
        pt_l = sb("pt_l", [128, PS, 2, NA], F32R, where=tctx)
        xn = sb("xn", [TT, HT, D], where=tctx)
        tctx.close()

        qblk = sb("qblk", [128, DT, IC, 2, T])
        kT = sb("kT", [128, DT, N])
        vT = sb("vT", [128, DT, N])
        vx = sb("vx", [TT, TC, HEADS, 2, VC])
        probs = sb("probs", [TT, 2, 2, DT, 2, T])
        smax = sb("smax", [TT, 2, 2 * DT * 2])
        probsT = sb("probsT", [TT, DT, PPM, TT])
        yrec = sb("yrec", [T, DT, 2 * PPM, 2])
        y = sb("y", [T, TC, 2, D])
        yT_h = sb("yT_h", [128, DT, N], F32R)
        yT_l = sb("yT_l", [128, DT, N], F32R)
        attnT = sb("attnT", [128, DT, N])
        stats2 = sb("stats2", [TT, TC, 6])
        mv2 = sb("mv2", [TT, TC, 2])
        var_eps2 = sb("var_eps2", [TT, TC])
        rstd2 = sb("rstd2", [TT, TC])
        xn2 = sb("xn2", [TT, TC, D])
        logitT = sb("logitT", [E, N])
        en = sb("en", [TT, TC, E])
        score = sb("score", [TT, TC, E])
        gsum6 = sb("gsum6", [TT, TC * N_GROUP, 6])
        gsum = sb("gsum", [TT, TC, N_GROUP])
        g_gt = sb("g_gt", [TT, TC, N_GROUP, N_GROUP])
        g_ge = sb("g_ge", [TT, TC, N_GROUP, N_GROUP])
        g_rank = sb("g_rank", [TT, TC, N_GROUP])
        g_in = sb("g_in", [TT, TC, N_GROUP])
        lower = sb("lower", [TT, N_GROUP, N_GROUP])
        masked = sb("masked", [TT, TC, E])
        top8 = sb("top8", [TT, TC, 8])
        above = sb("above", [TT, TC, E])
        n_above = sb("n_above", [TT, TC])
        PAD = 8
        run = [sb(f"run{i}", [TT, TC, PAD + E]) for i in range(2)]
        equal = sb("equal", [TT, TC, E])
        taken = sb("taken", [TT, TC, E])
        wsum = sb("wsum", [TT, TC])
        wrec = sb("wrec", [TT, TC])
        comb = sb("comb", [TT, TC, E])
        comb_r = sb("comb_r", [TT, TC, E], F32R)
        comb2 = sb("comb2", [TT, TC, 2, E])
        combT = sb("combT", [2 * E, N], F32R)
        th = sb("th", [128, 2, N])
        g1 = sb("g1", [128, 2, N])
        g2 = sb("g2", [128, 2, N])
        GR = 3
        g_h = sb("g_h", [128, GR, N], F32R)
        g_l = sb("g_l", [128, GR, N], F32R)
        ffnT = sb("ffnT", [128, DT, N])
        res = sb("res", [TT, TC, D])

        ps = ctx.enter_context(nc.psum_tensor("ps", [128, 8, 512], F32))

        ld_x = [sem(f"ld_x{i}") for i in range(2 * KT)]
        grouped = sem("grouped")
        ld_tokw, ld_attnw, ld_small, ld_gate = sem("ld_tokw"), sem("ld_attnw"), sem("ld_small"), sem("ld_gate")
        ld_unit = [sem(f"ld_unit{i}") for i in range(2 * NG)]
        pool_const = sem("pool_const")
        signs_done, alpha_done, pick_done = sem("signs_done"), sem("alpha_done"), sem("pick_done")
        signT_ps, signT_done = sem("signT_ps"), sem("signT_done")
        gateT_ps, gateT_h_done, gateT_done = sem("gateT_ps"), sem("gateT_h_done"), sem("gateT_done")
        tokw_h_done, tokw_done = sem("tokw_h_done"), sem("tokw_done")
        unit_h, unit_l = sem("unit_h"), sem("unit_l")
        patch_ps, patch_h, patch_l, patch_used = sem("patch_ps"), sem("patch_h"), sem("patch_l"), sem("patch_used")
        cls_done, emb_sb = sem("cls_done"), sem("emb_sb")
        tok_ps, tok_sb, aggr_done = sem("tok_ps"), sem("tok_sb"), sem("aggr_done")
        var_done, rstd_done, xn_done = sem("var_done"), sem("rstd_done"), sem("xn_done")
        xnT_ps, xnTh_done, xnTl_done = sem("xnT_ps"), sem("xnTh_done"), sem("xnTl_done")
        stats_done = sem("stats_done")
        p_done, max_done, yrec_done, h2_done = sem("p_done"), sem("max_done"), sem("yrec_done"), sem("h2_done")
        stats2_done, aggr2_done = sem("stats2_done"), sem("aggr2_done")
        var2_done, rstd2_done, xn2_done = sem("var2_done"), sem("rstd2_done"), sem("xn2_done")
        x2Th_done, yTh_done = sem("x2Th_done"), sem("yTh_done")
        route_step, comb_done = sem("route_step"), sem("comb_done")
        scores_half = sem("scores_half")
        u_ps, tanh_done, g1_done, w_ps, g2_done = sem("u_ps"), sem("tanh_done"), sem("g1_done"), sem("w_ps"), sem("g2_done")
        gh_done, gl_done, dn_used = sem("gh_done"), sem("gl_done"), sem("dn_used")
        ffn_sb, res_done, res_free = sem("ffn_sb"), sem("res_done"), sem("res_free")
        filled = [sem(f"filled{i}") for i in range(3)]
        emptied = [sem(f"emptied{i}") for i in range(3)]

        NTURN = 4 * DT

        def wait_gate(eng, c, u):
            if u < NSH:
                eng.wait_ge(g2_done, NU * c + u + 1)
            else:
                eng.wait_ge(g1_done, E * c + u - NSH + 1)

        def two_tiles(buffer, q):
            return buffer[:, :, q * 2 * TT:(q + 1) * 2 * TT].rearrange("p k (j t) -> p j k t", j=2)

        def chunk_tiles(buffer, c, q):
            return buffer[:, :, bass.ds(c * N + q * 2 * TT, 2 * TT)].rearrange("p k (j t) -> p j k t", j=2)

        registers = {}

        def wait_before(eng, once, least, semaphore, value):
            if eng not in registers:
                registers[eng] = eng.alloc_register(f"awaited{len(registers)}")
            eng.reg_mov(registers[eng], value)
            value = eng.snap(registers[eng])
            eng.wait_ge(once, least)
            eng.wait_ge(semaphore, value)

        PLAN = {0: ["qkv0", "qkv1", "qkv2"], 1: ["qkv3", "qkv4", "qkv5"], 2: ["v0", "v1"], 3: ["v2", "v3", "s0"],
                4: ["exp0"], 5: ["t0"], 6: ["y0", "s1"], 7: ["exp1"], 8: ["t1"], 9: ["y1", "s2"], 10: ["exp2"],
                11: ["t2"], 12: ["y2", "s3"], 13: ["exp3"], 14: ["t3"], 15: ["y3"], 16: ["yT0", "yT1"],
                17: ["proj0", "proj1"], 18: ["h0", "h1", "h2", "h3"], 19: ["stats"], 20: ["norm"],
                21: ["x0", "x1"]}
        SLOTS = NU + 2
        def jobs_of(step):
            kind = step.rstrip("0123456789")
            return [step + p for p in {"s": "ab", "t": "ab", "y": "ab"}.get(kind, " " * (kind not in ("exp", "stats", "norm")))]

        def order(attention, experts):
            found = []
            for k in range(SLOTS):
                if experts:
                    found += {0: ["logitT"], 1: ["logit"], NSH - 1: ["combT"]}.get(k, [])
                if attention:
                    found += [job.strip() for step in PLAN.get(k, []) for job in jobs_of(step)]
            return found + ["f0", "f1", "f2", "f3"] * experts

        FIRST, MIDDLE, LAST = order(True, False), order(True, True), order(False, True)
        assert len(MIDDLE) % 3 == 0

        def place(c, job):
            if isinstance(c, int) and c == 0:
                i = FIRST.index(job)
                return i % 3, i // 3
            i = len(FIRST) + (LAST if isinstance(c, int) and c == NC else MIDDLE).index(job)
            return i % 3, (c - 1) * (len(MIDDLE) // 3) + i // 3

        def wait_filled(eng, c, job):
            bank, before = place(c, job)
            eng.wait_ge(filled[bank], before + 1)

        def wait_emptied(eng, c, job):
            bank, before = place(c, job)
            eng.wait_ge(emptied[bank], before + 1)

        def wait_all_emptied(eng, c, jobs):
            last = {place(c, job)[0]: job for job in jobs}
            for job in last.values():
                wait_emptied(eng, c, job)

        def bank_of(c, job):
            return ps[:, 5 + place(c, job)[0]]

        block = ctx.enter_context(nc.Block())

        @block.sync
        def _(sp):
            xr = x.rearrange("b c (nh half py) w -> b c nh half (py w)", half=2, nh=NH)

            def load_x(n):
                g, k = divmod(n, KT)
                if n >= XS:
                    sp.wait_ge(grouped, n - XS + 1)
                src = xr[g * HALF:(g + 1) * HALF, k // 2, :, k % 2].rearrange("b r n -> b r n")
                sp.dma_start(xs[:, n % XS].rearrange("p y w -> p (y w)"), src).then_inc(ld_x[n], 16)

            load_x(0)
            sp.dma_start(tokw[:], tok_W.rearrange("(k p) d -> p k d", p=128)).then_inc(ld_tokw, 16)
            for n in range(1, XS):
                load_x(n)

            def load_unit(n):
                g, is_down = divmod(n, 2)
                if n >= RAW:
                    sp.wait_ge(unit_l, n - RAW + 1)
                slot = raw[:, n % RAW, :]
                if is_down:
                    dst = slot.rearrange("p (u d) -> p u d", u=UG)
                    src = (shared_down.rearrange("(u i) d -> i u d", i=I) if g == 0
                           else expert_down[(g - 1) * UG:g * UG].rearrange("u i d -> i u d"))
                    sp.dma_start(dst, src).then_inc(ld_unit[n], 16)
                elif g == 0:
                    for k in range(DT):
                        dst = slot.rearrange("p (u k i) -> p u k i", u=UG, k=DT)[:, :, k]
                        src = shared_up[k * 128:(k + 1) * 128].rearrange("p (u i) -> p u i", i=I)
                        sp.dma_start(dst, src).then_inc(ld_unit[n], 16)
                else:
                    dst = slot.rearrange("p (u i) -> p u i", u=UG * DT)
                    src = expert_up[(g - 1) * UG:g * UG].rearrange("u (k p) i -> p (u k) i", p=128)
                    sp.dma_start(dst, src).then_inc(ld_unit[n], 16)

            for n in range(XS, KT + XS):
                load_x(n)
            for n in range(NG):
                load_unit(n)
            for n in range(KT + XS, 2 * KT):
                load_x(n)
            for n in range(NG, 2 * NG):
                load_unit(n)
            sp.sem_inc(res_free, 16)
            for c in range(NC):
                sp.wait_ge(res_done, TC * c + TC)
                sp.dma_start(out_rows[c], res[:]).then_inc(res_free, 16)
            sp.wait_ge(res_free, 16 * NC + 16)

        @block.gpsimd
        def _(pool):
            steps = [0]

            def const(ins):
                ins.then_inc(pool_const, 1)
                steps[0] += 1
                pool.wait_ge(pool_const, steps[0])

            const(pool.memset(ident[:], 0.0))
            const(pool.affine_select(out=ident[:], in_=ident[:], compare_op=ALU.not_equal, fill=1.0, base=0,
                                     pattern=[[-1, 128]], channel_multiplier=1))
            const(pool.memset(parity_parts[:], 1.0))
            const(pool.affine_select(out=parity_parts[:], in_=parity_parts[:], compare_op=ALU.is_ge, fill=0.0,
                                     base=0, pattern=[[-DH, 2], [-2 * DH, PPM]], channel_multiplier=1))
            const(pool.affine_select(out=parity_parts[:], in_=parity_parts[:], compare_op=ALU.is_ge, fill=0.0,
                                     base=DH - 1, pattern=[[DH, 2], [2 * DH, PPM]], channel_multiplier=-1))
            const(pool.memset(image_of[:], 1.0))
            const(pool.affine_select(out=image_of[:], in_=image_of[:], compare_op=ALU.is_ge, fill=0.0,
                                     base=0, pattern=[[-T, 2]], channel_multiplier=1))
            const(pool.affine_select(out=image_of[:], in_=image_of[:], compare_op=ALU.is_ge, fill=0.0,
                                     base=T - 1, pattern=[[T, 2]], channel_multiplier=-1))
            const(pool.memset(minus_half[:], -0.5))
            const(pool.memset(pick0[:], 0.0))
            for part in range(2):
                const(pool.affine_select(out=pick0[:], in_=pick0[:], compare_op=ALU.not_equal, fill=1.0,
                                         base=-E * part, pattern=[[-1, E], [0, 128]], channel_multiplier=1))

            for g in range(2):
                pool.wait_ge(aggr_done, HT * (g + 1))
                pool.tensor_scalar(var_eps[:], mv[:, :, 1], EPS, None, ALU.add).then_inc(var_done, 1)
                pool.wait_ge(var_done, g + 1)
                if g:
                    pool.wait_ge(xn_done, HT * g)
                pool.tensor_tensor(rstd[:], var_eps[:], minus_half[:], ALU.pow).then_inc(rstd_done, 1)

            def variances(c):
                wait_before(pool, rstd_done, 2, aggr2_done, TC * c + TC)
                pool.tensor_scalar(var_eps2[:], mv2[:, :, 1], EPS, None, ALU.add).then_inc(var2_done, 1)
                pool.wait_ge(var2_done, c + 1)
                pool.tensor_tensor(rstd2[:], var_eps2[:], minus_half[:, 0:TC], ALU.pow).then_inc(rstd2_done, 1)

            variances(0)
            with pool.Fori(1, NC) as c:
                variances(c)

        @block.scalar
        def _(act):
            with nc.allow_non_contiguous_dma(reason="biases, a value per partition"):
                act.dma_start(tokb[:], tok_b.rearrange("(k p) -> p k", p=128)).then_inc(ld_small, 16)
                act.dma_start(clsT[:], cls_tok.rearrange("a b (k p) -> p (a b k)", p=128)).then_inc(ld_small, 16)
                for m, b in enumerate((bq, bk, bv, bp)):
                    act.dma_start(bias4[:, m], b.rearrange("(k p) -> p k", p=128)).then_inc(ld_small, 16)
            for m, w in enumerate((Wq, Wk, Wv, Wp)):
                act.dma_start(wraw[:, m], w.rearrange("(k p) c -> p k c", p=128)).then_inc(ld_attnw, 16)
            act.dma_start(gate_w[:], gate_W).then_inc(ld_gate, 16)

            act.wait_ge(ld_tokw, 16)
            act.activation(tokw_h[:], tokw[:], ACT.Copy).then_inc(tokw_h_done, 1)

            def split_patches(n):
                act.wait_ge(patch_ps, n + 1)
                if n == 0:
                    act.wait_ge(alpha_done, 1)
                if n >= PS:
                    act.wait_ge(patch_used, n - PS + 1)
                    act.wait_ge(patch_l, n - PS + 1)
                src = ps[:, 4 + 2 * (n % 2):6 + 2 * (n % 2), 0:NA]
                act.activation(pt_h[:, n % PS], src, ACT.Copy).then_inc(patch_h, 1)

            def signs():
                act.wait_ge(ld_attnw, 64)
                act.activation(wsign[:], wraw[:], ACT.Sign).then_inc(signs_done, 1)
                for n in range(NTURN):
                    act.wait_ge(signT_ps, n + 1)
                    m, ot = divmod(n, DT)
                    act.activation(signT[:, m, :, ot * 128:(ot + 1) * 128],
                                   ps[:, n % 4, 0:DT * 128].rearrange("p (k o) -> p k o", k=DT),
                                   ACT.Copy).then_inc(signT_done, 1)
                act.wait_ge(gateT_ps, 1)
                act.activation(gate_h[:], ps[:, 0, 0:DT * E].rearrange("p (k e) -> p k e", k=DT),
                               ACT.Copy).then_inc(gateT_h_done, 1)

            def unit_parts(n):
                g, is_down = divmod(n, 2)
                act.wait_ge(ld_unit[n], 32 if n == 0 else 16)
                dst = dn_h[:, g * UG:(g + 1) * UG] if is_down else up_h[:, g * UG:(g + 1) * UG]
                act.activation(dst.rearrange("p u d -> p (u d)") if is_down else dst.rearrange("p u k i -> p (u k i)"),
                               raw[:, n % RAW], ACT.Copy,
                               scale=0.5 if n == 1 else 1.0).then_inc(unit_h, 1)

            signs()
            for g in range(2):
                for k in range(KT):
                    split_patches(g * KT + k)
                act.wait_ge(patch_used, KT * (g + 1))
                act.wait_ge(ld_small, 96)
                if g:
                    act.wait_ge(tok_ps, HT * g)
                for dt in range(DT):
                    for w in range(2):
                        dst = hT[:, dt, :, 1:T].rearrange("p b (r w) -> p w b r", w=NW)[:, w * NPW:(w + 1) * NPW]
                        src = ps[:, 2 * dt + w, 0:NA].rearrange("p (w b r) -> p w b r", w=NPW, r=NH)
                        for i in range(NPW):
                            act.activation(dst[:, i], src[:, i], ACT.Identity,
                                           bias=tokb[:, dt:dt + 1]).then_inc(emb_sb, 1)
                for j in range(HT):
                    act.wait_ge(tok_ps, g * HT + j + 1)
                    act.activation(h_tok[:, g * HT + j], ps[0:TT, j % 4, 0:D], ACT.Copy).then_inc(tok_sb, 1)
                for n in range(NG * g, NG * (g + 1)):
                    unit_parts(n)
                for j in range(HT):
                    J = g * HT + j
                    act.wait_ge(xnT_ps, J + 1)
                    act.activation(xnT_h[:, :, J * TT:(J + 1) * TT],
                                   ps[:, j % 4, 0:DT * TT].rearrange("p (k t) -> p k t", k=DT),
                                   ACT.Copy).then_inc(xnTh_done, 1)

            def attention(c, step):
                kind, n = step.rstrip("0123456789"), int(step[-1]) if step[-1].isdigit() else 0
                if kind == "qkv" and n < DT:
                    wait_filled(act, c, step)
                    if n == 0:
                        act.wait_ge(alpha_done, 7)
                    bank, _ = place(c, step)
                    for a in range(2):
                        ins = act.activation(qblk[:, n, :, a, :],
                                             bank_of(c, step)[:, 0:N].rearrange("p (i t) -> p i t", t=T), ACT.Identity,
                                             scale=q_scale[:, n, a:a + 1], bias=q_bias[:, n, a:a + 1])
                    ins.then_inc(emptied[bank], 1)
                elif kind == "v":
                    wait_filled(act, c, step)
                    if n == 0:
                        act.wait_ge(route_step, 2 * TC)
                    bank, _ = place(c, step)
                    for i in range(2):
                        ins = act.activation(vx[:, n, :, i, 0:DH],
                                             bank_of(c, step)[0:TT, 0:D].rearrange("p (h d) -> p h d", d=DH), ACT.Copy,
                                             scale=image_of[:, i:i + 1])
                    ins.then_inc(emptied[bank], 1)
                elif kind == "exp":
                    wait_all_emptied(act, c, [f"s{n}a", f"s{n}b"])
                    p = probs[:].rearrange("p a b m i s -> p (a b m i s)")
                    act.activation(p, p, ACT.Exp).then_inc(p_done, 1)
                elif kind == "t":
                    if n:
                        wait_filled(act, c, f"y{n - 1}b")
                    for mt in range(DT):
                        job = step + "ab"[mt]
                        wait_filled(act, c, job)
                        act.activation(probsT[:, mt].rearrange("p r t -> p (r t)"),
                                       bank_of(c, job)[0:TT, 0:PPM * TT], ACT.Copy).then_inc(emptied[place(c, job)[0]], 1)
                elif kind == "yT":
                    wait_filled(act, c, step)
                    act.activation(two_tiles(yT_h, n), bank_of(c, step)[:, 0:N].rearrange("p (j k t) -> p j k t", j=2, k=DT),
                                   ACT.Copy).then_inc(yTh_done, 1)
                elif kind == "proj":
                    wait_filled(act, c, step)
                    act.activation(attnT[:, n], bank_of(c, step)[:, 0:N], ACT.Identity, scale=alpha[:, 3, n:n + 1],
                                   bias=bias4[:, 3, n:n + 1]).then_inc(emptied[place(c, step)[0]], 1)
                elif kind == "x":
                    bank, before = place(c, step)
                    wait_before(act, ld_small, 96, filled[bank], before + 1)
                    act.activation(chunk_tiles(xnT_h, c, n), bank_of(c, step)[:, 0:N].rearrange("p (j k t) -> p j k t", j=2, k=DT),
                                   ACT.Copy).then_inc(x2Th_done, 1)

            def high_part(f, u):
                act.wait_ge(g2_done, NU * f + u + 1)
                if u >= GR:
                    act.wait_ge(dn_used, NU * f + u - GR + 1)
                act.activation(g_h[:, u % GR], g2[:, u % 2], ACT.Copy).then_inc(gh_done, 1)

            def experts(c, k):
                f = c - 1
                if k < NU:
                    act.wait_ge(u_ps, NU * f + k + 1)
                    if k >= 2:
                        wait_gate(act, f, k - 2)
                    act.activation(th[:, k % 2], ps[:, 2 + k % 2, 0:N], ACT.Tanh, scale=0.5).then_inc(tanh_done, 1)
                if 1 <= k <= NU:
                    high_part(f, k - 1)
                if k == 0:
                    wait_filled(act, c, "logitT")
                    act.activation(logitT[:], bank_of(c, "logitT")[0:E, 0:N], ACT.Copy)\
                        .then_inc(emptied[place(c, "logitT")[0]], 1)
                if k == 1:
                    wait_filled(act, c, "logit")
                    act.activation(en[:], bank_of(c, "logit")[0:TT, 0:TC * E].rearrange("p (j e) -> p j e", e=E), ACT.Exp,
                                   scale=-1.0).then_inc(emptied[place(c, "logit")[0]], 1)
                if k == SLOTS - 1:
                    act.wait_ge(dn_used, NU * f + NU)
                    act.activation(ffnT[:], ps[:, 0:DT, 0:N], ACT.Copy).then_inc(ffn_sb, 1)

            def body(c, has_attention=True, has_experts=True):
                for k in range(SLOTS):
                    if has_experts:
                        experts(c, k)
                    if has_attention:
                        for step in PLAN.get(k, []):
                            attention(c, step)

            body(0, has_experts=False)
            with act.Fori(1, NC) as c:
                body(c)
            body(NC, has_attention=False)

        @block.vector
        def _(dve):
            dve.wait_ge(ld_attnw, 64)
            dve.tensor_reduce(alpha[:], wraw[:], AX.X, ALU.add, apply_absolute_value=True).then_inc(alpha_done, 1)
            dve.wait_ge(alpha_done, 1)
            dve.tensor_scalar(alpha[:], alpha[:], 1.0 / D, None, ALU.mult).then_inc(alpha_done, 1)
            dve.wait_ge(ld_tokw, 16)
            dve.wait_ge(tokw_h_done, 1)
            dve.tensor_tensor(tokw_l[:], tokw[:], tokw_h[:].bitcast(F32), ALU.subtract).then_inc(tokw_done, 1)
            dve.wait_ge(pool_const, 12)
            dve.tensor_reduce(parity[:], parity_parts[:], AX.X, ALU.add).then_inc(alpha_done, 1)
            dve.tensor_copy(pick_r[:], pick0[:]).then_inc(pick_done, 1)
            dve.wait_ge(alpha_done, 3)
            dve.wait_ge(ld_small, 96)
            for a in range(2):
                mask = parity[:, a:a + 1]
                dve.tensor_scalar(q_scale[:, :, a], alpha[:, 0], mask, SCALE, ALU.mult, ALU.mult).then_inc(alpha_done, 1)
                dve.tensor_scalar(q_bias[:, :, a], bias4[:, 0], mask, SCALE, ALU.mult, ALU.mult).then_inc(alpha_done, 1)
            dve.wait_ge(gateT_h_done, 1)
            dve.tensor_tensor(gate_l[:], ps[:, 0, 0:DT * E].rearrange("p (k e) -> p k e", k=DT),
                              gate_h[:].bitcast(F32), ALU.subtract).then_inc(gateT_done, 1)

            def unit_low(n):
                g, is_down = divmod(n, 2)
                dve.wait_ge(unit_h, n + 1)
                hi, lo = (dn_h, dn_l) if is_down else (up_h, up_l)
                flat = "p u d -> p (u d)" if is_down else "p u k i -> p (u k i)"
                hi = hi[:, g * UG:(g + 1) * UG].rearrange(flat)
                lo = lo[:, g * UG:(g + 1) * UG].rearrange(flat)
                dve.scalar_tensor_tensor(out=lo, in0=raw[:, n % RAW], scalar=0.5 if n == 1 else 1.0,
                                         in1=hi.bitcast(F32), op0=ALU.mult, op1=ALU.subtract).then_inc(unit_l, 1)

            def group_pixels(n):
                dve.wait_ge(ld_x[n], 16)
                if n >= 2:
                    dve.wait_ge(patch_ps, n - 1)
                dve.tensor_copy(xp[:, n % 2].rearrange("p w (y x) -> p w y x", x=P),
                                xs[:, n % XS].rearrange("p y (w x) -> p w y x", x=P)).then_inc(grouped, 1)

            group_pixels(0)
            for g in range(2):
                for k in range(KT):
                    n = g * KT + k
                    if n + 1 < 2 * KT:
                        group_pixels(n + 1)
                    dve.wait_ge(patch_h, n + 1)
                    if n >= PS:
                        dve.wait_ge(patch_used, n - PS + 1)
                    dve.tensor_tensor(pt_l[:, n % PS], ps[:, 4 + 2 * (n % 2):6 + 2 * (n % 2), 0:NA],
                                      pt_h[:, n % PS].bitcast(F32), ALU.subtract).then_inc(patch_l, 1)
                if g:
                    dve.wait_ge(tok_ps, HT * g)
                for dt in range(DT):
                    dve.tensor_copy(hT[:, dt, :, 0], clsT[:, dt:dt + 1].to_broadcast([128, HALF])).then_inc(cls_done, 1)
                for j in range(HT):
                    J = g * HT + j
                    dve.wait_ge(tok_sb, J + 1)
                    if g and j == 0:
                        dve.wait_ge(aggr_done, HT * g)
                    dve.bn_stats(stats[:, j], h_tok[:, J]).then_inc(stats_done, 1)
                if g:
                    dve.wait_ge(var_done, g)
                    dve.wait_ge(xn_done, HT * g)
                for j in range(HT):
                    dve.wait_ge(stats_done, g * HT + j + 1)
                    dve.bn_aggr(mv[:, j], stats[:, j]).then_inc(aggr_done, 1)
                dve.wait_ge(rstd_done, g + 1)
                dve.wait_ge(aggr_done, HT * (g + 1))
                for j in range(HT):
                    J = g * HT + j
                    if g:
                        dve.wait_ge(xnT_ps, HT * (g - 1) + j + 1)
                    dve.tensor_scalar(xn[:, j], h_tok[:, J], mv[:, j, 0:1], rstd[:, j:j + 1],
                                      ALU.subtract, ALU.mult).then_inc(xn_done, 1)
                for n in range(NG * g, NG * (g + 1)):
                    unit_low(n)
                for j in range(HT):
                    J = g * HT + j
                    dve.wait_ge(xnTh_done, J + 1)
                    dve.tensor_tensor(xnT_l[:, :, J * TT:(J + 1) * TT],
                                      ps[:, j % 4, 0:DT * TT].rearrange("p (k t) -> p k t", k=DT),
                                      xnT_h[:, :, J * TT:(J + 1) * TT].bitcast(F32),
                                      ALU.subtract).then_inc(xnTl_done, 1)

            dve.wait_ge(xnTl_done, NTILE)
            dve.wait_ge(unit_l, 2 * NG)
            dve.wait_ge(xnT_ps, NTILE)
            for i in range(2):
                for j in range(TC):
                    dve.tensor_copy(vx[:, j, :, i, DH], image_of[:, i:i + 1].to_broadcast([TT, HEADS])).then_inc(route_step, 1)
            for b in run:
                dve.memset(b[:, :, 0:PAD], 0.0).then_inc(route_step, 1)
            dve.memset(lower[:], 0.0).then_inc(route_step, 1)
            K0 = 2 * TC + 3
            dve.wait_ge(route_step, K0)
            for g in range(1, N_GROUP):
                dve.memset(lower[:, g, 0:g], 1.0).then_inc(route_step, 1)
            K0 += N_GROUP - 1
            dve.wait_ge(route_step, K0)

            STEPS = 28

            def attention(c, step):
                kind, n = step.rstrip("0123456789"), int(step[-1]) if step[-1].isdigit() else 0
                if kind == "qkv" and n >= DT:
                    m, mt = divmod(n, DT)
                    wait_filled(dve, c, step)
                    dve.tensor_scalar((kT, vT)[m - 1][:, mt], bank_of(c, step)[:, 0:N], alpha[:, m, mt:mt + 1],
                                      bias4[:, m, mt:mt + 1], ALU.mult, ALU.add).then_inc(emptied[place(c, step)[0]], 1)
                elif kind == "s":
                    for p in range(2):
                        job = step + "ab"[p]
                        S = bank_of(c, job)[0:TT, 0:2 * DT * TT].rearrange("p (g s) -> p g s", s=T)
                        wait_filled(dve, c, job)
                        dve.tensor_reduce(smax[:, p], S, AX.X, ALU.max).then_inc(max_done, 1)
                    for p in range(2):
                        job = step + "ab"[p]
                        S = bank_of(c, job)[0:TT, 0:2 * DT * TT].rearrange("p (g s) -> p g s", s=T)
                        dve.wait_ge(max_done, 2 * (TC * c + n) + p + 1)
                        dve.tensor_tensor(probs[:, p].rearrange("p b m i s -> p (b m i) s"), S,
                                          smax[:, p, :, None].to_broadcast([TT, 2 * DT * 2, T]),
                                          ALU.subtract).then_inc(emptied[place(c, job)[0]], 1)
                elif kind == "y":
                    for mt in range(DT):
                        job = step + "ab"[mt]
                        Y = bank_of(c, job)[0:T, 0:2 * PPM * 2 * VC].rearrange("p (h i v) -> p h i v", i=2, v=VC)
                        wait_filled(dve, c, job)
                        dve.reciprocal(yrec[:, mt], Y[:, :, :, DH]).then_inc(yrec_done, 1)
                    for mt in range(DT):
                        job = step + "ab"[mt]
                        Y = bank_of(c, job)[0:T, 0:2 * PPM * 2 * VC].rearrange("p (h i v) -> p h i v", i=2, v=VC)
                        dve.wait_ge(yrec_done, DT * (TC * c + n) + mt + 1)
                        dst = y[:, n].rearrange("p i (m h d) -> p m h i d", m=DT, d=DH)[:, mt]
                        dve.tensor_tensor(dst, Y[:, :, :, 0:DH], yrec[:, mt, :, :, None].to_broadcast([T, 2 * PPM, 2, DH]),
                                          ALU.mult).then_inc(emptied[place(c, job)[0]], 1)
                elif kind == "yT":
                    dve.wait_ge(yTh_done, 2 * c + n + 1)
                    dve.tensor_tensor(two_tiles(yT_l, n), bank_of(c, step)[:, 0:N].rearrange("p (j k t) -> p j k t", j=2, k=DT),
                                      two_tiles(yT_h, n).bitcast(F32), ALU.subtract).then_inc(emptied[place(c, step)[0]], 1)
                elif kind == "h":
                    wait_filled(dve, c, step)
                    row = h_tok[:, bass.ds(TC * c + n, 1), :].rearrange("p a d -> p (a d)")
                    dve.tensor_tensor(row, bank_of(c, step)[0:TT, 0:D], row, ALU.add).then_inc(emptied[place(c, step)[0]], 1)
                elif kind == "stats":
                    for j in range(TC):
                        bank, before = place(c, f"h{j}")
                        wait_before(dve, aggr_done, NTILE, emptied[bank], before + 1)
                        dve.bn_stats(stats2[:, j], h_tok[:, bass.ds(TC * c + j, 1), :].rearrange("p a d -> p (a d)"))\
                            .then_inc(stats2_done, 1)
                    for j in range(TC):
                        wait_before(dve, aggr_done, NTILE, stats2_done, TC * c + j + 1)
                        dve.bn_aggr(mv2[:, j], stats2[:, j]).then_inc(aggr2_done, 1)
                elif kind == "norm":
                    dve.wait_ge(aggr2_done, TC * c + TC)
                    dve.wait_ge(rstd2_done, c + 1)
                    for j in range(TC):
                        dve.tensor_scalar(xn2[:, j], h_tok[:, bass.ds(TC * c + j, 1), :].rearrange("p a d -> p (a d)"),
                                          mv2[:, j, 0:1], rstd2[:, j:j + 1],
                                          ALU.subtract, ALU.mult).then_inc(xn2_done, 1)
                elif kind == "x":
                    dve.wait_ge(x2Th_done, 2 * c + n + 1)
                    dve.tensor_tensor(chunk_tiles(xnT_l, c, n),
                                      bank_of(c, step)[:, 0:N].rearrange("p (j k t) -> p j k t", j=2, k=DT),
                                      chunk_tiles(xnT_h, c, n).bitcast(F32), ALU.subtract).then_inc(emptied[place(c, step)[0]], 1)

            def router(c):
                f = c - 1
                n = [0]

                def link(ins, before_max=False):
                    ins.then_inc(route_step, 1)
                    n[0] += 1
                    if before_max:
                        wait_before(dve, aggr_done, NTILE, route_step, f * STEPS + (K0 + n[0]))
                    else:
                        dve.wait_ge(route_step, f * STEPS + (K0 + n[0]))

                wait_emptied(dve, c, "logit")
                link(dve.tensor_scalar(en[:], en[:], 1.0, None, ALU.add))
                link(dve.reciprocal(score[:], en[:]))
                sc4 = score[:].rearrange("p j (g s) -> p (j g) s", s=GS)
                at = 0
                for d in range(1, GS):
                    ins = dve.tensor_tensor(gsum6[:, :, at:at + GS - d], sc4[:, :, 0:GS - d], sc4[:, :, d:GS], ALU.add)
                    at += GS - d
                    link(ins)
                link(dve.tensor_reduce(gsum[:].rearrange("p j g -> p (j g)"), gsum6[:], AX.X, ALU.max))
                for j in range(TC):
                    rival = gsum[:, j, None, :].to_broadcast([TT, N_GROUP, N_GROUP])
                    own = gsum[:, j, :, None].to_broadcast([TT, N_GROUP, N_GROUP])
                    dve.tensor_tensor(g_gt[:, j], rival, own, ALU.is_gt)
                    ins = dve.tensor_tensor(g_ge[:, j], rival, own, ALU.is_equal)
                link(ins)
                for j in range(TC):
                    ins = dve.tensor_tensor(g_ge[:, j], g_ge[:, j], lower[:], ALU.mult)
                link(ins)
                link(dve.tensor_tensor(g_gt[:], g_gt[:], g_ge[:], ALU.add))
                link(dve.tensor_reduce(g_rank[:].rearrange("p j g -> p (j g)"),
                                       g_gt[:].rearrange("p j g r -> p (j g) r"), AX.X, ALU.add))
                link(dve.tensor_scalar(g_in[:], g_rank[:], 1.5, None, ALU.is_lt))
                link(dve.tensor_tensor(masked[:].rearrange("p j (g s) -> p (j g) s", s=GS), sc4,
                                       g_in[:].rearrange("p j g -> p (j g)")[:, :, None].to_broadcast([TT, TC * N_GROUP, GS]),
                                       ALU.mult), before_max=True)
                for j in range(TC):
                    ins = dve.max(top8[:, j], masked[:, j])
                link(ins)
                kth = top8[:, :, TOP_K - 1:TOP_K].to_broadcast([TT, TC, E])
                dve.tensor_tensor(above[:], masked[:], kth, ALU.is_gt)
                dve.tensor_tensor(equal[:], masked[:], kth, ALU.is_equal)
                link(dve.tensor_tensor(run[0][:, :, PAD:], masked[:], kth, ALU.is_equal))
                link(dve.tensor_reduce(n_above[:], above[:], AX.X, ALU.add))
                for s in range(4):
                    a, b = run[s % 2], run[1 - s % 2]
                    link(dve.tensor_tensor(b[:, :, PAD:], a[:, :, PAD:], a[:, :, PAD - (1 << s):PAD - (1 << s) + E], ALU.add))
                link(dve.tensor_tensor(run[1][:, :, PAD:], run[0][:, :, PAD:],
                                       n_above[:, :, None].to_broadcast([TT, TC, E]), ALU.add))
                link(dve.tensor_scalar(run[1][:, :, PAD:], run[1][:, :, PAD:], TOP_K + 0.5, None, ALU.is_lt))
                link(dve.tensor_tensor(taken[:], run[1][:, :, PAD:], equal[:], ALU.mult))
                link(dve.tensor_tensor(taken[:], taken[:], above[:], ALU.add))
                link(dve.tensor_tensor(taken[:], taken[:], score[:], ALU.mult))
                link(dve.tensor_reduce(wsum[:], taken[:], AX.X, ALU.add))
                link(dve.tensor_scalar(wsum[:], wsum[:], 1e-20, None, ALU.add))
                link(dve.reciprocal(wrec[:], wsum[:]))
                link(dve.scalar_tensor_tensor(out=comb[:], in0=taken[:], scalar=0.5 * ROUTED,
                                              in1=wrec[:, :, None].to_broadcast([TT, TC, E]), op0=ALU.mult, op1=ALU.mult))
                assert n[0] == STEPS, n[0]
                dve.tensor_copy(comb_r[:], comb[:]).then_inc(comb_done, 1)
                dve.wait_ge(comb_done, 3 * f + 1)
                dve.tensor_copy(comb2[:, :, 0], comb_r[:].bitcast(F32)).then_inc(comb_done, 1)
                dve.tensor_tensor(comb2[:, :, 1], comb[:], comb_r[:].bitcast(F32), ALU.subtract).then_inc(comb_done, 1)

            def experts(c, k):
                f = c - 1
                if k < NU:
                    dve.wait_ge(tanh_done, NU * f + k + 1)
                    if k >= 2:
                        dve.wait_ge(gl_done, NU * f + k - 1)
                    gate = g2 if k < NSH else g1
                    ins = dve.scalar_tensor_tensor(out=gate[:, k % 2], in0=th[:, k % 2], scalar=1.0,
                                                   in1=ps[:, 2 + k % 2, 0:N], op0=ALU.add, op1=ALU.mult)
                    if k < NSH:
                        ins.then_inc(g2_done, 1)
                    else:
                        ins.then_inc(g1_done, 1)
                        dve.wait_ge(g1_done, E * f + k - NSH + 1)
                        dve.wait_ge(w_ps, E * f + k - NSH + 1)
                        dve.tensor_tensor(g2[:, k % 2], g1[:, k % 2], ps[:, 4, 0:N], ALU.mult).then_inc(g2_done, 1)
                if 1 <= k <= NU:
                    u = k - 1
                    dve.wait_ge(gh_done, NU * f + u + 1)
                    dve.tensor_tensor(g_l[:, u % GR], g2[:, u % 2], g_h[:, u % GR].bitcast(F32),
                                      ALU.subtract).then_inc(gl_done, 1)
                if k == 1:
                    router(c)
                if k == NSH - 1:
                    wait_filled(dve, c, "combT")
                    dve.tensor_copy(combT[:], bank_of(c, "combT")[0:2 * E, 0:N]).then_inc(emptied[place(c, "combT")[0]], 1)

            def finish(c):
                dve.wait_ge(res_free, 16 * c)
                for j in range(TC):
                    wait_filled(dve, c, f"f{j}")
                    dve.tensor_tensor(res[:, j], bank_of(c, f"f{j}")[0:TT, 0:D],
                                      h_tok[:, bass.ds(TC * (c - 1) + j, 1), :].rearrange("p a d -> p (a d)"),
                                      ALU.add).then_inc(emptied[place(c, f"f{j}")[0]], 1)
                wait_emptied(dve, c, f"f{TC - 1}")
                dve.engine_nop().then_inc(res_done, TC)

            def body(c, has_attention=True, has_experts=True):
                for k in range(SLOTS):
                    if has_experts:
                        experts(c, k)
                    if has_attention:
                        for step in PLAN.get(k, []):
                            attention(c, step)
                if has_experts:
                    finish(c)

            body(0, has_experts=False)
            with dve.Fori(1, NC) as c:
                body(c)
            body(NC, has_attention=False)

        @block.tensor
        def _(pe):
            pe.wait_ge(pool_const, 2)
            pe.wait_ge(signs_done, 1)
            for n in range(NTURN):
                m, ot = divmod(n, DT)
                if n >= 4:
                    pe.wait_ge(signT_done, n - 3)
                for kt in range(DT):
                    mm = pe.transpose(ps[:, n % 4, kt * 128:(kt + 1) * 128], wsign[:, m, ot, kt * 128:(kt + 1) * 128], ident[:])
                mm.then_inc(signT_ps, 1)
            pe.wait_ge(ld_gate, 16)
            pe.wait_ge(signT_done, NTURN)
            for kt in range(DT):
                mm = pe.transpose(ps[:, 0, kt * E:(kt + 1) * E], gate_w[:, kt * 128:(kt + 1) * 128], ident[0:E, 0:E])
            mm.then_inc(gateT_ps, 1)

            def turn_patches(n):
                g, k = divmod(n, KT)
                pe.wait_ge(grouped, n + 1)
                if n >= 2:
                    pe.wait_ge(patch_l, n - 1)
                for w in range(NW):
                    src = xp[:, n % 2, w]
                    mm = pe.transpose(ps[:, 4 + 2 * (n % 2) + w // NPW, (w % NPW) * RH:(w % NPW + 1) * RH], src,
                                      ident[0:RH, 0:RH])
                mm.then_inc(patch_ps, 1)

            def embed(n):
                g, k = divmod(n, KT)
                pe.wait_ge(tokw_done, 1)
                pe.wait_ge(patch_l, n + 1)
                if k == 0:
                    pe.wait_ge(gateT_done, 1)
                    if g:
                        pe.wait_ge(xnTl_done, HT * g)
                for dt in range(DT):
                    for w in range(2):
                        for i, (a, b) in enumerate(((tokw_h, pt_h), (tokw_h, pt_l), (tokw_l, pt_h))):
                            mm = pe.matmul(ps[:, 2 * dt + w, 0:NA], a[:, k, dt * 128:(dt + 1) * 128], b[:, n % PS, w],
                                           start=(k == 0 and i == 0), stop=(k == KT - 1 and i == 2))
                mm.then_inc(patch_used, 1)

            for g in range(2):
                if g == 0:
                    turn_patches(0)
                for k in range(KT):
                    n = g * KT + k
                    if n + 1 < 2 * KT:
                        turn_patches(n + 1)
                    embed(n)
                pe.wait_ge(emb_sb, 2 * DT * NPW * (g + 1))
                pe.wait_ge(cls_done, DT * (g + 1))
                for j in range(HT):
                    if j >= 4:
                        pe.wait_ge(tok_sb, g * HT + j - 3)
                    for dt in range(DT):
                        src = hT[:, dt].rearrange("p b t -> p (b t)")[:, j * TT:(j + 1) * TT]
                        mm = pe.transpose(ps[0:TT, j % 4, dt * 128:(dt + 1) * 128], src, ident[:])
                    mm.then_inc(tok_ps, 1)
                pe.wait_ge(tok_sb, HT * (g + 1))
                for j in range(HT):
                    pe.wait_ge(xn_done, g * HT + j + 1)
                    if j >= 4:
                        pe.wait_ge(xnTl_done, g * HT + j - 3)
                    for kt in range(DT):
                        mm = pe.transpose(ps[:, j % 4, kt * TT:(kt + 1) * TT], xn[:, j, kt * 128:(kt + 1) * 128],
                                          ident[0:TT, 0:TT])
                    mm.then_inc(xnT_ps, 1)

            pe.wait_ge(xnTl_done, NTILE)
            pe.wait_ge(unit_l, 2 * NG)
            def start(c, job, made_of=()):
                bank, before = place(c, job)
                wait_all_emptied(pe, c, [source for source in made_of if place(c, source)[0] != bank])
                pe.wait_ge(emptied[bank], before)
                return bank_of(c, job)

            def attention(c, step):
                kind, n = step.rstrip("0123456789"), int(step[-1]) if step[-1].isdigit() else 0
                if kind == "qkv":
                    m, mt = divmod(n, DT)
                    out_ps = start(c, step)
                    for kt in range(DT):
                        for i, b in enumerate((xnT_h, xnT_l)):
                            mm = pe.matmul(out_ps[:, 0:N], signT[:, m, kt, mt * 128:(mt + 1) * 128],
                                           b[:, kt, bass.ds(N * c, N)], start=(kt == 0 and i == 0),
                                           stop=(kt == DT - 1 and i == 1))
                    mm.then_inc(filled[place(c, step)[0]], 1)
                elif kind == "v":
                    out_ps = start(c, step, ["qkv4", "qkv5"] if n == 0 else [])
                    for mt in range(DT):
                        mm = pe.transpose(out_ps[0:TT, mt * 128:(mt + 1) * 128], vT[:, mt, n * TT:(n + 1) * TT], ident[:])
                    mm.then_inc(filled[place(c, step)[0]], 1)
                elif kind == "s":
                    qk = [f"qkv{i}" for i in range(2 * DT)] if n == 0 else []
                    banks = [start(c, step + "a", qk), start(c, step + "b")]
                    for r in range(PPM):
                        rows = slice(32 * r, 32 * r + 32)
                        if r == 2:
                            pe.wait_ge(scores_half, 2 * (TC * c + n + 1))
                        for mt in range(DT):
                            for i in range(2):
                                img = 2 * n + i
                                at = (r // 2 * DT + mt) * TT + i * T
                                mm = pe.matmul(banks[r % 2][0:TT, at:at + T],
                                               qblk[rows, mt, img].rearrange("p a t -> p (a t)"),
                                               kT[rows, mt, img * T:(img + 1) * T], start=True, stop=True)
                        if r < 2:
                            mm.then_inc(scores_half, 1)
                        else:
                            mm.then_inc(filled[place(c, step + "ab"[r % 2])[0]], 1)
                elif kind == "t":
                    pe.wait_ge(p_done, TC * c + n + 1)
                    for mt in range(DT):
                        job = step + "ab"[mt]
                        out_ps = start(c, job)
                        for r in range(PPM):
                            mm = pe.transpose(out_ps[0:TT, r * TT:(r + 1) * TT],
                                              probs[:, r % 2, r // 2, mt].rearrange("p i s -> p (i s)"), ident[0:TT, 0:TT])
                        mm.then_inc(filled[place(c, job)[0]], 1)
                elif kind == "y":
                    for mt in range(DT):
                        job = step + "ab"[mt]
                        out_ps = start(c, job, [f"v{j}" for j in range(TC)] * (n == 0) + [f"t{n}" + "ab"[mt]])
                        for h in range(2 * PPM):
                            mm = pe.matmul(out_ps[0:T, h * 2 * VC:(h + 1) * 2 * VC],
                                           probsT[:, mt, h // 2, h % 2 * T:(h % 2 + 1) * T],
                                           vx[:, n, mt * 2 * PPM + h].rearrange("p i v -> p (i v)"),
                                           start=True, stop=True)
                        mm.then_inc(filled[place(c, job)[0]], 1)
                elif kind == "yT":
                    wait_all_emptied(pe, c, [f"y{j}{p}" for j in (2 * n, 2 * n + 1) for p in "ab"])
                    bank, before = place(c, step)
                    wait_before(pe, pool_const, 2, emptied[bank], before)
                    for j in range(2):
                        for mt in range(DT):
                            for i in range(2):
                                at = (j * DT + mt) * TT + i * T
                                mm = pe.transpose(bank_of(c, step)[:, at:at + T],
                                                  y[:, 2 * n + j, i, mt * 128:(mt + 1) * 128], ident[0:T, 0:T])
                    mm.then_inc(filled[place(c, step)[0]], 1)
                elif kind == "proj":
                    out_ps = start(c, step, ["yT0", "yT1"] if n == 0 else [])
                    for kt in range(DT):
                        for i, b in enumerate((yT_h, yT_l)):
                            mm = pe.matmul(out_ps[:, 0:N], signT[:, 3, kt, n * 128:(n + 1) * 128], b[:, kt],
                                           start=(kt == 0 and i == 0), stop=(kt == DT - 1 and i == 1))
                    mm.then_inc(filled[place(c, step)[0]], 1)
                elif kind == "h":
                    out_ps = start(c, step, ["proj0", "proj1"] if n == 0 else [])
                    for ot in range(DT):
                        mm = pe.transpose(out_ps[0:TT, ot * 128:(ot + 1) * 128], attnT[:, ot, n * TT:(n + 1) * TT], ident[:])
                    mm.then_inc(filled[place(c, step)[0]], 1)
                elif kind == "x":
                    pe.wait_ge(xn2_done, TC * c + 2 * n + 2)
                    out_ps = start(c, step)
                    for j in range(2):
                        for kt in range(DT):
                            at = (j * DT + kt) * TT
                            mm = pe.transpose(out_ps[:, at:at + TT], xn2[:, 2 * n + j, kt * 128:(kt + 1) * 128],
                                              ident[0:TT, 0:TT])
                    mm.then_inc(filled[place(c, step)[0]], 1)

            def experts(c, k):
                f = c - 1
                tokens = bass.ds(N * f, N)
                if k == 0:
                    out_ps = start(c, "logitT")
                    for kt in range(DT):
                        for i, (a, b) in enumerate(((gate_h, xnT_h), (gate_h, xnT_l), (gate_l, xnT_h))):
                            mm = pe.matmul(out_ps[0:E, 0:N], a[:, kt], b[:, kt, tokens],
                                           start=(kt == 0 and i == 0), stop=(kt == DT - 1 and i == 2))
                    mm.then_inc(filled[place(c, "logitT")[0]], 1)
                if k == 1:
                    bank, before = place(c, "logit")
                    wait_emptied(pe, c, "logitT")
                    wait_before(pe, pool_const, 2, emptied[bank], before)
                    out_ps = bank_of(c, "logit")
                    for j in range(TC):
                        mm = pe.transpose(out_ps[0:TT, j * E:(j + 1) * E], logitT[:, j * TT:(j + 1) * TT], ident[0:E, 0:E])
                    mm.then_inc(filled[place(c, "logit")[0]], 1)
                if k < NU:
                    if k >= 2:
                        wait_gate(pe, f, k - 2)
                    for kt in range(DT):
                        for i, (a, b) in enumerate(((up_h, xnT_h), (up_h, xnT_l), (up_l, xnT_h))):
                            mm = pe.matmul(ps[:, 2 + k % 2, 0:N], a[:, k, kt], b[:, kt, tokens],
                                           start=(kt == 0 and i == 0), stop=(kt == DT - 1 and i == 2))
                    mm.then_inc(u_ps, 1)
                if k == NSH - 1:
                    pe.wait_ge(comb_done, 3 * f + 3)
                    out_ps = start(c, "combT")
                    for j in range(TC):
                        mm = pe.transpose(out_ps[0:2 * E, j * TT:(j + 1) * TT],
                                          comb2[:, j].rearrange("p a e -> p (a e)"), ident[0:TT, 0:TT])
                    mm.then_inc(filled[place(c, "combT")[0]], 1)
                if NSH <= k < NU:
                    e = k - NSH
                    if e == 0:
                        wait_emptied(pe, c, "combT")
                    else:
                        pe.wait_ge(g2_done, NU * f + k)
                    pe.matmul(ps[:, 4, 0:N], pick_r[:, e], combT[:], start=True, stop=True).then_inc(w_ps, 1)
                if k >= 2:
                    u = k - 2
                    pe.wait_ge(gl_done, NU * f + u + 1)
                    for dt in range(DT):
                        w = slice(dt * 128, (dt + 1) * 128)
                        for i, (a, b) in enumerate(((dn_h, g_h), (dn_h, g_l), (dn_l, g_h))):
                            mm = pe.matmul(ps[:, dt, 0:N], a[:, u, w], b[:, u % GR],
                                           start=(u == 0 and i == 0), stop=(u == NU - 1 and i == 2))
                    mm.then_inc(dn_used, 1)

            def body(c, has_attention=True, has_experts=True):
                for k in range(SLOTS):
                    if has_experts:
                        experts(c, k)
                    if has_attention:
                        for step in PLAN.get(k, []):
                            attention(c, step)
                if has_experts:
                    pe.wait_ge(ffn_sb, c)
                    for j in range(TC):
                        out_ps = start(c, f"f{j}")
                        for dt in range(DT):
                            mm = pe.transpose(out_ps[0:TT, dt * 128:(dt + 1) * 128], ffnT[:, dt, j * TT:(j + 1) * TT], ident[:])
                        mm.then_inc(filled[place(c, f"f{j}")[0]], 1)
                if has_attention:
                    wait_all_emptied(pe, c, ["x0", "x1"])

            body(0, has_experts=False)
            with pe.Fori(1, NC) as c:
                body(c)
            body(NC, has_attention=False)


_INS = ["x", "cls_tok", "L0_tok_W", "L0_tok_b", "L0_attn_Wq", "L0_attn_bq", "L0_attn_Wk", "L0_attn_bk",
        "L0_attn_Wv", "L0_attn_bv", "L0_attn_Wp", "L0_attn_bp", "L0_ffn_gate_weight", "L0_ffn_expert_up",
        "L0_ffn_expert_down", "L0_ffn_shared_up", "L0_ffn_shared_down"]


def kernel(**inputs):
    import concourse.bacc as bacc
    from concourse.bass_utils import run_bass_kernel_spmd

    nc = bacc.Bacc("TRN2", target_bir_lowering=False, num_devices=1)
    arrays, args = {}, []
    for name in _INS:
        a = np.ascontiguousarray(inputs[name])
        arrays[f"in_{name}"] = a
        args.append(nc.dram_tensor(f"in_{name}", a.shape, F32, kind="ExternalInput").ap())
    B, _, H, W = inputs["x"].shape
    D = inputs["L0_tok_W"].shape[1]
    shape = (B, (H // 16) * (W // 16) + 1, D)
    args.append(nc.dram_tensor("out_h", shape, F32, kind="ExternalOutput").ap())
    vit_block(nc, *args)
    r = run_bass_kernel_spmd(nc, [arrays], core_ids=[0])
    return r.results[0]["out_h"]
```

```python
from contextlib import ExitStack

import numpy as np

import concourse.bass as bass
from concourse import mybir

F32 = mybir.dt.float32
F32R = mybir.dt.float32r
ACT = mybir.ActivationFunctionType
ALU = mybir.AluOpType
AX = mybir.AxisListType


def vit_block(nc, x, cls_tok, tok_W, tok_b, Wq, bq, Wk, bk, Wv, bv, Wp, bp,
              gate_W, expert_up, expert_down, shared_up, shared_down, out):
    B, CH, IMH, IMW = x.shape
    P = 16
    D = tok_W.shape[1]
    NH, NW = IMH // P, IMW // P
    T = NH * NW + 1
    E, _, I = expert_up.shape
    IS = shared_up.shape[1]
    HEADS, TOP_K, N_GROUP = 16, 4, 4
    DH = D // HEADS
    GS = E // N_GROUP
    DT = D // 128
    KT = CH * P * P // 128
    TT = 2 * T
    NTILE = B // 2
    NC = 4
    IC = B // NC
    TC = NTILE // NC
    N = IC * T
    RC = IC * NH
    NP = NW * RC
    NSH = IS // I
    NU = E + NSH
    UG = 4
    NG = NU // UG
    PPM = 4
    VC = DH + 1
    EPS = 1e-5
    SCALE = float(DH) ** -0.5
    ROUTED = 2.5

    out_rows = out.rearrange("b t d -> (b t) d").rearrange("(c j p) d -> c p j d", c=NC, p=TT)

    ctx = ExitStack()
    with ctx:
        def sb(name, shape, dt=F32, where=ctx):
            return where.enter_context(nc.sbuf_tensor(name, shape, dt))

        def sem(name):
            return ctx.enter_context(nc.semaphore(name))

        ident = sb("ident", [128, 128])
        parity = sb("parity", [128, 2])
        parity_parts = sb("parity_parts", [128, 2, PPM])
        image_of = sb("image_of", [TT, 2])
        pick_r = sb("pick_r", [2 * E, E, 128], F32R)
        minus_half = sb("minus_half", [TT, TC])
        up_h = sb("up_h", [128, NU, DT, I], F32R)
        signT = sb("signT", [128, 4, DT, D], F32R)
        alpha = sb("alpha", [128, 4, DT])
        bias4 = sb("bias4", [128, 4, DT])
        q_scale = sb("q_scale", [128, DT, 2])
        q_bias = sb("q_bias", [128, DT, 2])
        tokb = sb("tokb", [128, DT])
        clsT = sb("clsT", [128, DT])
        gate_h = sb("gate_h", [128, DT, E], F32R)
        gate_l = sb("gate_l", [128, DT, E], F32R)
        h_tok = sb("h_tok", [TT, NTILE, D])
        xnT_h = sb("xnT_h", [128, DT, NTILE * TT], F32R)
        xnT_l = sb("xnT_l", [128, DT, NTILE * TT], F32R)

        with ExitStack() as early:
            pick0 = sb("pick0", [2 * E, E, 128], where=early)
        y = sb("y", [T, TC, 2, D])
        yT_h = sb("yT_h", [128, DT, N], F32R)
        yT_l = sb("yT_l", [128, DT, N], F32R)
        attnT = sb("attnT", [128, DT, N])
        qblk = sb("qblk", [128, DT, IC, 2, T])
        kT = sb("kT", [128, DT, N])
        vT = sb("vT", [128, DT, N])
        vx = sb("vx", [TT, TC, HEADS, 2, VC])
        probs = sb("probs", [TT, 2, 2, 2, DT, 2, T])
        smax = sb("smax", [TT, 2, 2 * DT * 2])
        probsT = sb("probsT", [TT, 2, DT, PPM, TT])
        yrec = sb("yrec", [T, DT, 2 * PPM, 2])
        stats2 = sb("stats2", [TT, TC, 6])
        mv2 = sb("mv2", [TT, TC, 2])
        var_eps2 = sb("var_eps2", [TT, TC])
        rstd2 = sb("rstd2", [TT, TC])
        xn2 = sb("xn2", [TT, TC, D])
        logitT = sb("logitT", [E, N])
        en = sb("en", [TT, TC, E])
        lower = sb("lower", [TT, N_GROUP, N_GROUP])
        PAD = 8
        run = [sb(f"run{i}", [TT, TC, PAD + E]) for i in range(2)]

        RAW = 3
        with ExitStack() as early:
            wsign = sb("wsign", [128, 4, DT, D], where=early)
            raw = sb("raw", [128, RAW, UG * DT * I], where=early)
        th = sb("th", [128, 2, N])
        g1 = sb("g1", [128, 2, N])
        g2 = sb("g2", [128, 2, N])
        GR = 3
        g_h = sb("g_h", [128, GR, N], F32R)
        g_l = sb("g_l", [128, GR, N], F32R)
        ffnT = sb("ffnT", [128, DT, N])
        res = sb("res", [TT, TC, D])
        score = sb("score", [TT, TC, E])
        gsum6 = sb("gsum6", [TT, TC * N_GROUP, 6])
        gsum = sb("gsum", [TT, TC, N_GROUP])
        g_gt = sb("g_gt", [TT, TC, N_GROUP, N_GROUP])
        g_ge = sb("g_ge", [TT, TC, N_GROUP, N_GROUP])
        g_rank = sb("g_rank", [TT, TC, N_GROUP])
        g_in = sb("g_in", [TT, TC, N_GROUP])
        masked = sb("masked", [TT, TC, E])
        top8 = sb("top8", [TT, TC, 8])
        above = sb("above", [TT, TC, E])
        n_above = sb("n_above", [TT, TC])
        equal = sb("equal", [TT, TC, E])
        taken = sb("taken", [TT, TC, E])
        wsum = sb("wsum", [TT, TC])
        wrec = sb("wrec", [TT, TC])
        comb = sb("comb", [TT, TC, E])
        comb_r = sb("comb_r", [TT, TC, E], F32R)
        comb2 = sb("comb2", [TT, TC, 2, E])
        combT = sb("combT", [2 * E, N], F32R)

        XS, XP, PS = 3, 3, 3
        with ExitStack() as early:
            tokw = sb("tokw", [128, KT, D], where=early)
            wraw = sb("wraw", [128, 4, DT, D], where=early)
            gate_w = sb("gate_w", [E, D], where=early)
            xs = sb("xs", [RC, XS, P // 2, IMW], where=early)
            xp = sb("xp", [RC, XP, NW, P // 2 * P], where=early)
            tokw_h = sb("tokw_h", [128, KT, D], F32R, where=early)
            tokw_l = sb("tokw_l", [128, KT, D], F32R, where=early)
            pt_h = sb("pt_h", [128, PS, NP], F32R, where=early)
            pt_l = sb("pt_l", [128, PS, NP], F32R, where=early)
            hT = sb("hT", [128, 2, DT, IC, T], where=early)
            stats = sb("stats", [TT, TC, 6], where=early)
            mv = sb("mv", [TT, TC, 2], where=early)
            var_eps = sb("var_eps", [TT, TC], where=early)
            rstd = sb("rstd", [TT, TC], where=early)
            xn = sb("xn", [TT, TC, D], where=early)
        up_l = sb("up_l", [128, NU, DT, I], F32R)
        dn_h = sb("dn_h", [128, NU, D], F32R)
        dn_l = sb("dn_l", [128, NU, D], F32R)

        ps = ctx.enter_context(nc.psum_tensor("ps", [128, 8, 512], F32))

        ld_x = [sem(f"ld_x{i}") for i in range(NC * KT)]
        grouped = sem("grouped")
        ld_attnw, ld_small, ld_gate = sem("ld_attnw"), sem("ld_small"), sem("ld_gate")
        ld_tokw = [sem(f"ld_tokw{i}") for i in range(2)]
        ld_unit = [sem(f"ld_unit{i}") for i in range(2 * NG)]
        pool_const = sem("pool_const")
        signs_done, alpha_done, pick_done = sem("signs_done"), sem("alpha_done"), sem("pick_done")
        signT_ps, signT_done = sem("signT_ps"), sem("signT_done")
        gateT_ps, gateT_h_done, gateT_done = sem("gateT_ps"), sem("gateT_h_done"), sem("gateT_done")
        tokw_h_done, tokw_done = sem("tokw_h_done"), sem("tokw_done")
        unit_h = sem("unit_h")
        unit_l = [sem("unit_l_pool"), sem("unit_l_dve")]
        patch_ps, patch_h, patch_l, patch_used = sem("patch_ps"), sem("patch_h"), sem("patch_l"), sem("patch_used")
        cls_done, emb_sb = sem("cls_done"), sem("emb_sb")
        tok_ps, tok_sb, aggr_done = sem("tok_ps"), sem("tok_sb"), sem("aggr_done")
        var_done, rstd_done, xn_done = sem("var_done"), sem("rstd_done"), sem("xn_done")
        xnT_ps, xnTh_done, xnTl_done = sem("xnT_ps"), sem("xnTh_done"), sem("xnTl_done")
        stats_done = sem("stats_done")
        p_done, max_done, yrec_done, h2_done = sem("p_done"), sem("max_done"), sem("yrec_done"), sem("h2_done")
        stats2_done, aggr2_done = sem("stats2_done"), sem("aggr2_done")
        var2_done, rstd2_done, xn2_done = sem("var2_done"), sem("rstd2_done"), sem("xn2_done")
        x2Th_done, yTh_done = sem("x2Th_done"), sem("yTh_done")
        route_step, comb_done = sem("route_step"), sem("comb_done")
        scores_half = sem("scores_half")
        u_ps, tanh_done, g1_done, w_ps, g2_done = sem("u_ps"), sem("tanh_done"), sem("g1_done"), sem("w_ps"), sem("g2_done")
        gh_done, gl_done, dn_used = sem("gh_done"), sem("gl_done"), sem("dn_used")
        ffn_sb, res_done, res_free = sem("ffn_sb"), sem("res_done"), sem("res_free")
        filled = [sem(f"filled{i}") for i in range(3)]
        emptied = [sem(f"emptied{i}") for i in range(3)]

        NTURN = 4 * DT

        def wait_gate(eng, c, u):
            if u < NSH:
                eng.wait_ge(g2_done, NU * c + u + 1)
            else:
                eng.wait_ge(g1_done, E * c + u - NSH + 1)

        def two_tiles(buffer, q):
            return buffer[:, :, q * 2 * TT:(q + 1) * 2 * TT].rearrange("p k (j t) -> p j k t", j=2)

        def chunk_tiles(buffer, c, q):
            return buffer[:, :, bass.ds(c * N + q * 2 * TT, 2 * TT)].rearrange("p k (j t) -> p j k t", j=2)

        registers = {}

        def wait_before(eng, once, least, semaphore, value):
            if eng not in registers:
                registers[eng] = eng.alloc_register(f"awaited{len(registers)}")
            eng.reg_mov(registers[eng], value)
            value = eng.snap(registers[eng])
            eng.wait_ge(once, least)
            eng.wait_ge(semaphore, value)

        FIRST_STEPS = ["qkv0", "qkv1", "qkv2", "qkv3", "qkv4", "qkv5"]
        PLAN = {0: ["v0", "v1", "v2"], 1: ["v3", "s0", "z0"], 2: ["exp0"], 3: ["s1", "z1"], 4: ["t0", "exp1"],
                5: ["y0"], 6: ["s2", "z2"], 7: ["t1"], 8: ["exp2", "y1"], 9: ["s3"], 10: ["z3"],
                11: ["t2", "exp3", "y2"], 12: ["t3"], 13: ["yT0", "y3"], 14: ["yT1"], 15: ["proj0"], 16: ["proj1"],
                17: ["h0", "h1", "h2", "h3", "stats", "next0", "next1"], 19: ["norm", "next2", "next3", "x0"],
                20: ["x1", "next4", "next5"], 21: ["logitT"]}
        FIRST_PLAN = {0: ["v0"], 1: ["v1", "v2", "v3", "s0"], 2: ["z0"], 3: ["exp0", "s1"], 5: ["z1"], 7: ["t0"],
                      8: ["exp1", "s2"], 9: ["z2"], 10: ["y0", "t1", "exp2", "s3", "z3", "y1", "exp3", "t2"],
                      11: ["y2", "t3"], 14: ["y3", "yT0"], 15: ["yT1"], 16: ["proj0", "proj1", "h0", "next0"],
                      17: ["next1", "h1", "h2", "h3", "next2", "stats"], 18: ["norm", "next3"],
                      19: ["next4", "next5"], 20: ["x0", "x1", "logitT"]}
        LAST_STEPS = ["logit"]
        ROUTE = {-1: [0, 1], 0: [2], 1: [3]}
        SLOTS = NU + 2
        POOL_CONSTANTS = 12
        EARLY_PIECES = 3
        WEIGHT_PIECES = [(g, False) for g in range(EARLY_PIECES)] + [(g, True) for g in range(EARLY_PIECES)]
        WEIGHT_PIECES += [(g, is_down) for g in range(EARLY_PIECES, NG) for is_down in (False, True)]
        EARLY_LOADS = [14 + 3 * i for i in range(EARLY_PIECES)]
        assert EARLY_PIECES * UG * DT * I <= KT * D + 4 * DT * D
        PROLOGUE = [(0, "piece", 0), (0, "piece", 1), (0, "piece", 2), (0, "sign", 0), (0, "piece", 3),
                    (0, "sign", 1), (0, "piece", 4), (0, "piece", 5), (0, "sign", 2), (0, "class", 0), (0, "sign", 3),
                    (0, "alpha", 0), (0, "signT", 0), (0, "tok", 0), (1, "piece", 0), (0, "signT", 1), (0, "tok", 1),
                    (0, "stats", 0), (1, "piece", 1), (0, "signT", 2), (0, "norm", 0), (1, "piece", 2),
                    (0, "signT", 3), (0, "turn", 0), (0, "gateT", 0), (1, "piece", 3), (0, "turn", 1),
                    (1, "piece", 4)]
        TOK_PLAN = {-1: [(1, "piece", 5)], 0: [(2, "piece", 0), (1, "tok", 0)], 1: [(2, "piece", 1)],
                    2: [(1, "tok", 1), (2, "piece", 2)], 3: [(1, "stats", 0)],
                    4: [(2, "piece", 3), (2, "piece", 4), (1, "norm", 0), (1, "turn", 0), (2, "piece", 5), (1, "turn", 1)],
                    5: [(3, "piece", 0), (2, "tok", 0)],
                    6: [(2, "tok", 1), (3, "piece", 1), (3, "piece", 2), (2, "stats", 0), (3, "piece", 3)],
                    7: [(2, "norm", 0), (3, "piece", 4)], 8: [(2, "turn", 0)], 9: [(2, "turn", 1), (3, "piece", 5)],
                    10: [(3, "tok", 0), (3, "tok", 1)], 11: [(3, "stats", 0)],
                    12: [(3, "norm", 0), (3, "turn", 0), (3, "turn", 1)]}
        TOK_SLOTS = max(TOK_PLAN) + 1
        UNIT_PLAN = {1: [0], 3: [1], 5: [2], 12: [3], 13: [4], 14: [5], 15: [6], 17: [7], 18: [8], 19: [9]}
        CONSTANTS_SLOT = 3
        VAR_UNIT = 18

        def jobs_of(step):
            kind = step.rstrip("0123456789")
            if kind in ("z", "exp", "stats", "norm"):
                return []
            return [step + "a", step + "b"] if kind in ("s", "t", "y") else [step]

        def steps(c, k):
            plan = FIRST_PLAN if isinstance(c, int) and c == 0 else PLAN
            last = isinstance(c, int) and c == NC - 1
            return [step for step in plan.get(k, []) if not (last and step.startswith("next"))]

        def order(c, attention, experts):
            found = [job for step in FIRST_STEPS * (not experts) for job in jobs_of(step)]
            for k in range(SLOTS):
                if experts:
                    found += ["combT"] * (k == NSH - 1)
                if attention:
                    found += [job for step in steps(c, k) for job in jobs_of(step)]
            return found + ["f0", "f1", "f2", "f3"] * experts + LAST_STEPS * attention

        MIDDLE = order(None, True, True)
        ORDERS = ([order(0, True, False)] + [MIDDLE] * (NC - 2) + [order(NC - 1, True, True), order(NC, False, True)])
        assert len(MIDDLE) % 3 == 0

        def job_number(c, i):
            if isinstance(c, int):
                i += sum(len(jobs) for jobs in ORDERS[:c])
                return i % 3, i // 3
            i += len(ORDERS[0])
            return i % 3, (c - 1) * (len(MIDDLE) // 3) + i // 3

        def place(c, job):
            return job_number(c, (ORDERS[c] if isinstance(c, int) else MIDDLE).index(job))

        def wait_filled(eng, c, job):
            bank, before = place(c, job)
            eng.wait_ge(filled[bank], before + 1)

        def wait_emptied(eng, c, job):
            bank, before = place(c, job)
            eng.wait_ge(emptied[bank], before + 1)

        def wait_all_emptied(eng, c, jobs):
            last = {place(c, job)[0]: job for job in jobs}
            for job in last.values():
                wait_emptied(eng, c, job)

        def bank_of(c, job):
            return ps[:, 5 + place(c, job)[0]]

        def unit_low(eng, n):
            g, is_down = WEIGHT_PIECES[n]
            if n < 2:
                eng.wait_ge(tokw_done, 2)
                eng.wait_ge(alpha_done, 1)
                eng.wait_ge(signs_done, 4)
                eng.wait_ge(gateT_ps, 1)
            eng.wait_ge(unit_h, n + 1)
            hi, lo = (dn_h, dn_l) if is_down else (up_h, up_l)
            flat = "p u d -> p (u d)" if is_down else "p u k i -> p (u k i)"
            hi = hi[:, g * UG:(g + 1) * UG].rearrange(flat).bitcast(F32)
            lo = lo[:, g * UG:(g + 1) * UG].rearrange(flat)
            if (g, is_down) == (0, True):
                ins = eng.scalar_tensor_tensor(out=lo, in0=raw[:, n % RAW], scalar=0.5, in1=hi, op0=ALU.mult, op1=ALU.subtract)
            else:
                ins = eng.tensor_tensor(lo, raw[:, n % RAW], hi, ALU.subtract)
            ins.then_inc(unit_l[n % 2], 1)

        block = ctx.enter_context(nc.Block())

        @block.sync
        def _(sp):
            xr = x.rearrange("b c (nh half py) w -> b c nh half (py w)", half=2, nh=NH)

            def load_x(n):
                c, k = divmod(n, KT)
                if n >= XS:
                    sp.wait_ge(grouped, n - XS + 1)
                src = xr[c * IC:(c + 1) * IC, k // 2, :, k % 2].rearrange("b r n -> b r n")
                sp.dma_start(xs[:, n % XS].rearrange("p y w -> p (y w)"), src).then_inc(ld_x[n], 16)

            load_x(0)
            for half in range(2):
                k = slice(half * KT // 2, (half + 1) * KT // 2)
                sp.dma_start(tokw[:, k], tok_W.rearrange("(k p) d -> p k d", p=128)[:, k]).then_inc(ld_tokw[half], 16)
                load_x(1 + half)
            for n in range(3, XS):
                load_x(n)
            load_x(3)
            for m, w in enumerate((Wq, Wk, Wv, Wp)):
                sp.dma_start(wraw[:, m], w.rearrange("(k p) c -> p k c", p=128)).then_inc(ld_attnw, 16)
            load_x(4)
            with nc.allow_non_contiguous_dma(reason="biases, a value per partition"):
                sp.dma_start(tokb[:], tok_b.rearrange("(k p) -> p k", p=128)).then_inc(ld_small, 16)
                sp.dma_start(clsT[:], cls_tok.rearrange("a b (k p) -> p (a b k)", p=128)).then_inc(ld_small, 16)
                for m, b in enumerate((bq, bk, bv, bp)):
                    sp.dma_start(bias4[:, m], b.rearrange("(k p) -> p k", p=128)).then_inc(ld_small, 16)
            sp.dma_start(gate_w[:], gate_W).then_inc(ld_gate, 16)

            def load_unit(n):
                g, is_down = WEIGHT_PIECES[n]
                if n == 0:
                    sp.wait_ge(signT_ps, NTURN)
                if n >= RAW:
                    sp.wait_ge(unit_l[(n - RAW) % 2], (n - RAW) // 2 + 1)
                slot = raw[:, n % RAW, :]
                if is_down:
                    dst = slot.rearrange("p (u d) -> p u d", u=UG)
                    src = (shared_down.rearrange("(u i) d -> i u d", i=I) if g == 0
                           else expert_down[(g - 1) * UG:g * UG].rearrange("u i d -> i u d"))
                    sp.dma_start(dst, src).then_inc(ld_unit[n], 16)
                elif g == 0:
                    for k in range(DT):
                        dst = slot.rearrange("p (u k i) -> p u k i", u=UG, k=DT)[:, :, k]
                        src = shared_up[k * 128:(k + 1) * 128].rearrange("p (u i) -> p u i", i=I)
                        sp.dma_start(dst, src).then_inc(ld_unit[n], 16)
                else:
                    dst = slot.rearrange("p (u i) -> p u i", u=UG * DT)
                    src = expert_up[(g - 1) * UG:g * UG].rearrange("u (k p) i -> p (u k) i", p=128)
                    sp.dma_start(dst, src).then_inc(ld_unit[n], 16)

            for n in range(XS + 2, NC * KT):
                load_x(n)
                if n in EARLY_LOADS:
                    load_unit(EARLY_LOADS.index(n))
            for n in range(EARLY_PIECES, 2 * NG):
                load_unit(n)
            sp.sem_inc(res_free, 16)
            for c in range(NC):
                sp.wait_ge(res_done, TC * c + TC)
                sp.dma_start(out_rows[c], res[:]).then_inc(res_free, 16)
            sp.wait_ge(res_free, 16 * NC + 16)

        @block.gpsimd
        def _(pool):
            made = [0]

            def const(ins):
                ins.then_inc(pool_const, 1)
                made[0] += 1
                pool.wait_ge(pool_const, made[0])

            const(pool.memset(ident[:], 0.0))
            const(pool.affine_select(out=ident[:], in_=ident[:], compare_op=ALU.not_equal, fill=1.0, base=0,
                                     pattern=[[-1, 128]], channel_multiplier=1))
            const(pool.memset(parity_parts[:], 1.0))
            const(pool.affine_select(out=parity_parts[:], in_=parity_parts[:], compare_op=ALU.is_ge, fill=0.0,
                                     base=0, pattern=[[-DH, 2], [-2 * DH, PPM]], channel_multiplier=1))
            const(pool.affine_select(out=parity_parts[:], in_=parity_parts[:], compare_op=ALU.is_ge, fill=0.0,
                                     base=DH - 1, pattern=[[DH, 2], [2 * DH, PPM]], channel_multiplier=-1))
            const(pool.memset(image_of[:], 1.0))
            const(pool.affine_select(out=image_of[:], in_=image_of[:], compare_op=ALU.is_ge, fill=0.0,
                                     base=0, pattern=[[-T, 2]], channel_multiplier=1))
            const(pool.affine_select(out=image_of[:], in_=image_of[:], compare_op=ALU.is_ge, fill=0.0,
                                     base=T - 1, pattern=[[T, 2]], channel_multiplier=-1))
            const(pool.memset(minus_half[:], -0.5))
            const(pool.memset(pick0[:], 0.0))
            for part in range(2):
                const(pool.affine_select(out=pick0[:], in_=pick0[:], compare_op=ALU.not_equal, fill=1.0,
                                         base=-E * part, pattern=[[-1, E], [0, 128]], channel_multiplier=1))

            def tokens(c, kind, n):
                if kind == "norm":
                    pool.wait_ge(aggr_done, TC * c + TC)
                    pool.tensor_scalar(var_eps[:], mv[:, :, 1], EPS, None, ALU.add).then_inc(var_done, 1)
                    pool.wait_ge(var_done, c + 1)
                    if c:
                        pool.wait_ge(xn_done, TC * c)
                    pool.tensor_tensor(rstd[:], var_eps[:], minus_half[:], ALU.pow).then_inc(rstd_done, 1)

            for step in PROLOGUE:
                tokens(*step)
            assert made[0] == POOL_CONSTANTS

            def variances(c):
                wait_before(pool, rstd_done, NC, aggr2_done, TC * c + TC)
                pool.tensor_scalar(var_eps2[:], mv2[:, :, 1], EPS, None, ALU.add).then_inc(var2_done, 1)
                pool.wait_ge(var2_done, c + 1)
                pool.tensor_tensor(rstd2[:], var_eps2[:], minus_half[:], ALU.pow).then_inc(rstd2_done, 1)

            def low_part(f, u):
                pool.wait_ge(gh_done, NU * f + u + 1)
                pool.tensor_tensor(g_l[:, u % GR], g2[:, u % 2], g_h[:, u % GR].bitcast(F32),
                                   ALU.subtract).then_inc(gl_done, 1)

            for k in range(-1, SLOTS):
                for step in TOK_PLAN.get(k, []):
                    tokens(*step)
                if "stats" in FIRST_PLAN.get(k, []):
                    variances(0)
                for n in UNIT_PLAN.get(k, []):
                    if n % 2 == 0:
                        unit_low(pool, n)
            with pool.Fori(1, NC) as c:
                for u in range(VAR_UNIT):
                    low_part(c - 1, u)
                variances(c)
                for u in range(VAR_UNIT, NU):
                    low_part(c - 1, u)
            for u in range(NU):
                low_part(NC - 1, u)

        @block.scalar
        def _(act):
            def signs(m):
                if m == 0:
                    act.wait_ge(ld_attnw, 64)
                act.activation(wsign[:, m], wraw[:, m], ACT.Sign).then_inc(signs_done, 1)

            def turned_signs(n):
                act.wait_ge(signT_ps, n + 1)
                m, ot = divmod(n, DT)
                act.activation(signT[:, m, :, ot * 128:(ot + 1) * 128],
                               ps[:, 5 + n % 3, 0:DT * 128].rearrange("p (k o) -> p k o", k=DT),
                               ACT.Copy).then_inc(signT_done, 1)

            def unit_parts(n):
                g, is_down = WEIGHT_PIECES[n]
                act.wait_ge(ld_unit[n], 32 if n == 0 else 16)
                if n == EARLY_PIECES:
                    act.wait_ge(xnTl_done, 2 * NC)
                dst = dn_h[:, g * UG:(g + 1) * UG] if is_down else up_h[:, g * UG:(g + 1) * UG]
                act.activation(dst.rearrange("p u d -> p (u d)") if is_down else dst.rearrange("p u k i -> p (u k i)"),
                               raw[:, n % RAW], ACT.Copy,
                               scale=0.5 if (g, is_down) == (0, True) else 1.0).then_inc(unit_h, 1)

            def high_patches(n):
                act.wait_ge(patch_ps, n + 1)
                if n >= PS:
                    act.wait_ge(patch_used, n - PS + 1)
                    act.wait_ge(patch_l, n - PS + 1)
                act.activation(pt_h[:, n % PS], ps[:, 2 + n % 2, 0:NP], ACT.Copy).then_inc(patch_h, 1)

            def tokens(c, kind, n):
                if kind == "piece":
                    n = c * KT + n
                    if n + 1 < NC * KT:
                        high_patches(n + 1)
                    if n % KT == KT - 1:
                        act.wait_ge(patch_used, n + 1)
                        if c == 0:
                            act.wait_ge(ld_small, 96)
                        if c >= 2:
                            act.wait_ge(tok_ps, 2 * (c - 1))
                        for dt in range(DT):
                            dst = hT[:, c % 2, dt, :, 1:T].rearrange("p b (r w) -> p w b r", w=NW)
                            src = ps[:, dt, 0:NP].rearrange("p (w b r) -> p w b r", w=NW, r=NH)
                            act.activation(dst, src, ACT.Identity, bias=tokb[:, dt:dt + 1]).then_inc(emb_sb, 1)
                elif kind == "sign":
                    signs(n)
                elif kind == "signT":
                    turned_signs(2 * n)
                    turned_signs(2 * n + 1)
                elif kind == "gateT":
                    act.wait_ge(gateT_ps, 1)
                    act.activation(gate_h[:], ps[:, 5 + NTURN % 3, 0:DT * E].rearrange("p (k e) -> p k e", k=DT),
                                   ACT.Copy).then_inc(gateT_h_done, 1)
                elif kind == "tok":
                    act.wait_ge(tok_ps, 2 * c + n + 1)
                    j = TC * c + 2 * n
                    act.activation(h_tok[:, j:j + 2], ps[0:TT, 4, 0:2 * D].rearrange("p (j d) -> p j d", j=2),
                                   ACT.Copy).then_inc(tok_sb, 1)
                elif kind == "turn":
                    act.wait_ge(xnT_ps, 2 * c + n + 1)
                    act.activation(chunk_tiles(xnT_h, c, n), ps[:, 4, 0:N].rearrange("p (j k t) -> p j k t", j=2, k=DT),
                                   ACT.Copy).then_inc(xnTh_done, 1)

            high_patches(0)
            for i, half in enumerate((slice(0, KT // 2), slice(KT // 2, KT))):
                act.wait_ge(ld_tokw[i], 16)
                act.activation(tokw_h[:, half], tokw[:, half], ACT.Copy).then_inc(tokw_h_done, 1)
            for step in PROLOGUE:
                tokens(*step)

            def attention(c, step):
                kind, n = step.rstrip("0123456789"), int(step[-1]) if step[-1].isdigit() else 0
                if kind in ("qkv", "next") and n < DT:
                    wait_filled(act, c, step)
                    if step == "qkv0":
                        act.wait_ge(alpha_done, 7)
                    bank, _ = place(c, step)
                    for a in range(2):
                        ins = act.activation(qblk[:, n, :, a, :],
                                             bank_of(c, step)[:, 0:N].rearrange("p (i t) -> p i t", t=T), ACT.Identity,
                                             scale=q_scale[:, n, a:a + 1], bias=q_bias[:, n, a:a + 1])
                    ins.then_inc(emptied[bank], 1)
                elif kind == "next":
                    m, mt = divmod(n, DT)
                    wait_filled(act, c, step)
                    act.activation((kT, vT)[m - 1][:, mt], bank_of(c, step)[:, 0:N], ACT.Identity, scale=alpha[:, m, mt:mt + 1],
                                   bias=bias4[:, m, mt:mt + 1]).then_inc(emptied[place(c, step)[0]], 1)
                elif kind == "v":
                    wait_filled(act, c, step)
                    bank, _ = place(c, step)
                    for i in range(2):
                        ins = act.activation(vx[:, n, :, i, 0:DH],
                                             bank_of(c, step)[0:TT, 0:D].rearrange("p (h d) -> p h d", d=DH), ACT.Copy,
                                             scale=image_of[:, i:i + 1])
                    ins.then_inc(emptied[bank], 1)
                elif kind == "exp":
                    wait_all_emptied(act, c, [f"s{n}a", f"s{n}b"])
                    p = probs[:, n % 2].rearrange("p a b m i s -> p (a b m i s)")
                    act.activation(p, p, ACT.Exp).then_inc(p_done, 1)
                elif kind == "t":
                    if n >= 2:
                        wait_filled(act, c, f"y{n - 2}b")
                    for mt in range(DT):
                        job = step + "ab"[mt]
                        wait_filled(act, c, job)
                        act.activation(probsT[:, n % 2, mt].rearrange("p r t -> p (r t)"),
                                       bank_of(c, job)[0:TT, 0:PPM * TT], ACT.Copy).then_inc(emptied[place(c, job)[0]], 1)
                elif kind == "yT":
                    wait_filled(act, c, step)
                    act.activation(two_tiles(yT_h, n), bank_of(c, step)[:, 0:N].rearrange("p (j k t) -> p j k t", j=2, k=DT),
                                   ACT.Copy).then_inc(yTh_done, 1)
                elif kind == "proj":
                    wait_filled(act, c, step)
                    act.activation(attnT[:, n], bank_of(c, step)[:, 0:N], ACT.Identity, scale=alpha[:, 3, n:n + 1],
                                   bias=bias4[:, 3, n:n + 1]).then_inc(emptied[place(c, step)[0]], 1)
                elif kind == "x":
                    bank, before = place(c, step)
                    wait_before(act, ld_small, 96, filled[bank], before + 1)
                    act.activation(chunk_tiles(xnT_h, c, n), bank_of(c, step)[:, 0:N].rearrange("p (j k t) -> p j k t", j=2, k=DT),
                                   ACT.Copy).then_inc(x2Th_done, 1)

                elif kind == "logitT":
                    wait_filled(act, c, step)
                    act.activation(logitT[:], bank_of(c, step)[0:E, 0:N], ACT.Copy).then_inc(emptied[place(c, step)[0]], 1)
                elif kind == "logit":
                    wait_filled(act, c, step)
                    act.activation(en[:], bank_of(c, step)[0:TT, 0:TC * E].rearrange("p (j e) -> p j e", e=E), ACT.Exp,
                                   scale=-1.0).then_inc(emptied[place(c, step)[0]], 1)

            def high_part(f, u):
                act.wait_ge(g2_done, NU * f + u + 1)
                if u >= GR:
                    act.wait_ge(dn_used, NU * f + u - GR + 1)
                act.activation(g_h[:, u % GR], g2[:, u % 2], ACT.Copy).then_inc(gh_done, 1)

            def experts(c, k):
                f = c - 1
                if k < NU:
                    act.wait_ge(u_ps, NU * f + k + 1)
                    if k >= 2:
                        wait_gate(act, f, k - 2)
                    act.activation(th[:, k % 2], ps[:, 2 + k % 2, 0:N], ACT.Tanh, scale=0.5).then_inc(tanh_done, 1)
                if 1 <= k <= NU:
                    high_part(f, k - 1)
                if k == SLOTS - 1:
                    act.wait_ge(dn_used, NU * f + NU)
                    act.activation(ffnT[:], ps[:, 0:DT, 0:N], ACT.Copy).then_inc(ffn_sb, 1)

            def body(c, has_attention=True, has_experts=True):
                if not has_experts:
                    for step in FIRST_STEPS:
                        attention(c, step)
                if not has_experts:
                    for step in TOK_PLAN.get(-1, []):
                        tokens(*step)
                for k in range(SLOTS):
                    if has_experts:
                        experts(c, k)
                    for step in TOK_PLAN.get(k, []) if not has_experts else []:
                        tokens(*step)
                    if has_attention:
                        for step in steps(c, k):
                            attention(c, step)
                    for n in UNIT_PLAN.get(k, []) if not has_experts else []:
                        unit_parts(n)
                if has_attention:
                    for step in LAST_STEPS:
                        attention(c, step)

            body(0, has_experts=False)
            with act.Fori(1, NC - 1) as c:
                body(c)
            body(NC - 1)
            body(NC, has_attention=False)

        @block.vector
        def _(dve):
            def attention_constants():
                dve.wait_ge(ld_attnw, 64)
                dve.tensor_reduce(alpha[:], wraw[:], AX.X, ALU.add, apply_absolute_value=True).then_inc(alpha_done, 1)
                dve.wait_ge(alpha_done, 1)
                dve.tensor_scalar(alpha[:], alpha[:], 1.0 / D, None, ALU.mult).then_inc(alpha_done, 1)
                dve.wait_ge(pool_const, 12)
                dve.tensor_reduce(parity[:], parity_parts[:], AX.X, ALU.add).then_inc(alpha_done, 1)
                dve.wait_ge(alpha_done, 3)
                dve.wait_ge(ld_small, 96)
                for a in range(2):
                    mask = parity[:, a:a + 1]
                    dve.tensor_scalar(q_scale[:, :, a], alpha[:, 0], mask, SCALE, ALU.mult, ALU.mult).then_inc(alpha_done, 1)
                    dve.tensor_scalar(q_bias[:, :, a], bias4[:, 0], mask, SCALE, ALU.mult, ALU.mult).then_inc(alpha_done, 1)

            def gate_low():
                dve.wait_ge(gateT_h_done, 1)
                dve.tensor_tensor(gate_l[:], ps[:, 5 + NTURN % 3, 0:DT * E].rearrange("p (k e) -> p k e", k=DT),
                                  gate_h[:].bitcast(F32), ALU.subtract).then_inc(gateT_done, 1)

            def group_pixels(n):
                dve.wait_ge(ld_x[n], 16)
                if n >= XP:
                    dve.wait_ge(patch_ps, n - XP + 1)
                dve.tensor_copy(xp[:, n % XP].rearrange("p w (y x) -> p w y x", x=P),
                                xs[:, n % XS].rearrange("p y (w x) -> p w y x", x=P)).then_inc(grouped, 1)

            def low_patches(n):
                dve.wait_ge(patch_h, n + 1)
                if n >= PS:
                    dve.wait_ge(patch_used, n - PS + 1)
                dve.tensor_tensor(pt_l[:, n % PS], ps[:, 2 + n % 2, 0:NP], pt_h[:, n % PS].bitcast(F32),
                                  ALU.subtract).then_inc(patch_l, 1)

            def tokens(c, kind, n):
                if kind == "piece":
                    n = c * KT + n
                    if n + 1 < NC * KT:
                        low_patches(n + 1)
                    if n + 3 < NC * KT:
                        group_pixels(n + 3)
                elif kind == "class":
                    dve.wait_ge(ld_small, 96)
                    for slot in range(2):
                        for dt in range(DT):
                            dve.tensor_copy(hT[:, slot, dt, :, 0], clsT[:, dt:dt + 1].to_broadcast([128, IC])).then_inc(cls_done, 1)
                elif kind == "alpha":
                    attention_constants()
                elif kind == "gateT":
                    gate_low()
                elif kind == "stats":
                    for j in range(TC):
                        dve.wait_ge(tok_sb, 2 * c + j // 2 + 1)
                        if c and j == 0:
                            dve.wait_ge(aggr_done, TC * c)
                        dve.bn_stats(stats[:, j], h_tok[:, TC * c + j]).then_inc(stats_done, 1)
                    if c:
                        dve.wait_ge(var_done, c)
                        dve.wait_ge(xn_done, TC * c)
                    for j in range(TC):
                        dve.wait_ge(stats_done, TC * c + j + 1)
                        dve.bn_aggr(mv[:, j], stats[:, j]).then_inc(aggr_done, 1)
                elif kind == "norm":
                    dve.wait_ge(rstd_done, c + 1)
                    dve.wait_ge(aggr_done, TC * c + TC)
                    if c:
                        dve.wait_ge(xnT_ps, 2 * c)
                    for j in range(TC):
                        dve.tensor_scalar(xn[:, j], h_tok[:, TC * c + j], mv[:, j, 0:1], rstd[:, j:j + 1],
                                          ALU.subtract, ALU.mult).then_inc(xn_done, 1)
                elif kind == "turn":
                    dve.wait_ge(xnTh_done, 2 * c + n + 1)
                    dve.tensor_tensor(chunk_tiles(xnT_l, c, n), ps[:, 4, 0:N].rearrange("p (j k t) -> p j k t", j=2, k=DT),
                                      chunk_tiles(xnT_h, c, n).bitcast(F32), ALU.subtract).then_inc(xnTl_done, 1)

            for n in range(3):
                group_pixels(n)
                if n == 0:
                    low_patches(0)
            for half in range(2):
                dve.wait_ge(tokw_h_done, half + 1)
                k = slice(half * KT // 2, (half + 1) * KT // 2)
                dve.tensor_tensor(tokw_l[:, k], tokw[:, k], tokw_h[:, k].bitcast(F32), ALU.subtract).then_inc(tokw_done, 1)
            for step in PROLOGUE:
                tokens(*step)

            K0 = 2 * TC + 2 + N_GROUP

            def chunk_constants():
                dve.wait_ge(pool_const, POOL_CONSTANTS)
                dve.tensor_copy(pick_r[:], pick0[:]).then_inc(pick_done, 1)
                for i in range(2):
                    for j in range(TC):
                        dve.tensor_copy(vx[:, j, :, i, DH], image_of[:, i:i + 1].to_broadcast([TT, HEADS])).then_inc(route_step, 1)
                for b in run:
                    dve.memset(b[:, :, 0:PAD], 0.0).then_inc(route_step, 1)
                dve.memset(lower[:], 0.0).then_inc(route_step, 1)
                dve.wait_ge(route_step, K0 - N_GROUP + 1)
                for g in range(1, N_GROUP):
                    dve.memset(lower[:, g, 0:g], 1.0).then_inc(route_step, 1)
                dve.wait_ge(route_step, K0)

            STEPS = 28

            def attention(c, step):
                kind, n = step.rstrip("0123456789"), int(step[-1]) if step[-1].isdigit() else 0
                if kind == "qkv" and n >= DT:
                    m, mt = divmod(n, DT)
                    wait_filled(dve, c, step)
                    dve.tensor_scalar((kT, vT)[m - 1][:, mt], bank_of(c, step)[:, 0:N], alpha[:, m, mt:mt + 1],
                                      bias4[:, m, mt:mt + 1], ALU.mult, ALU.add).then_inc(emptied[place(c, step)[0]], 1)
                elif kind == "z":
                    step = f"s{n}"
                    for p in range(2):
                        job = step + "ab"[p]
                        S = bank_of(c, job)[0:TT, 0:2 * DT * TT].rearrange("p (g s) -> p g s", s=T)
                        wait_filled(dve, c, job)
                        dve.tensor_reduce(smax[:, p], S, AX.X, ALU.max).then_inc(max_done, 1)
                    for p in range(2):
                        job = step + "ab"[p]
                        S = bank_of(c, job)[0:TT, 0:2 * DT * TT].rearrange("p (g s) -> p g s", s=T)
                        dve.wait_ge(max_done, 2 * (TC * c + n) + p + 1)
                        dve.tensor_tensor(probs[:, n % 2, p].rearrange("p b m i s -> p (b m i) s"), S,
                                          smax[:, p, :, None].to_broadcast([TT, 2 * DT * 2, T]),
                                          ALU.subtract).then_inc(emptied[place(c, job)[0]], 1)
                elif kind == "y":
                    for mt in range(DT):
                        job = step + "ab"[mt]
                        Y = bank_of(c, job)[0:T, 0:2 * PPM * 2 * VC].rearrange("p (h i v) -> p h i v", i=2, v=VC)
                        wait_filled(dve, c, job)
                        dve.reciprocal(yrec[:, mt], Y[:, :, :, DH]).then_inc(yrec_done, 1)
                    for mt in range(DT):
                        job = step + "ab"[mt]
                        Y = bank_of(c, job)[0:T, 0:2 * PPM * 2 * VC].rearrange("p (h i v) -> p h i v", i=2, v=VC)
                        dve.wait_ge(yrec_done, DT * (TC * c + n) + mt + 1)
                        dst = y[:, n].rearrange("p i (m h d) -> p m h i d", m=DT, d=DH)[:, mt]
                        dve.tensor_tensor(dst, Y[:, :, :, 0:DH], yrec[:, mt, :, :, None].to_broadcast([T, 2 * PPM, 2, DH]),
                                          ALU.mult).then_inc(emptied[place(c, job)[0]], 1)
                elif kind == "yT":
                    dve.wait_ge(yTh_done, 2 * c + n + 1)
                    dve.tensor_tensor(two_tiles(yT_l, n), bank_of(c, step)[:, 0:N].rearrange("p (j k t) -> p j k t", j=2, k=DT),
                                      two_tiles(yT_h, n).bitcast(F32), ALU.subtract).then_inc(emptied[place(c, step)[0]], 1)
                elif kind == "h":
                    wait_filled(dve, c, step)
                    row = h_tok[:, bass.ds(TC * c + n, 1), :].rearrange("p a d -> p (a d)")
                    dve.tensor_tensor(row, bank_of(c, step)[0:TT, 0:D], row, ALU.add).then_inc(emptied[place(c, step)[0]], 1)
                elif kind == "stats":
                    for j in range(TC):
                        bank, before = place(c, f"h{j}")
                        wait_before(dve, aggr_done, NTILE, emptied[bank], before + 1)
                        dve.bn_stats(stats2[:, j], h_tok[:, bass.ds(TC * c + j, 1), :].rearrange("p a d -> p (a d)"))\
                            .then_inc(stats2_done, 1)
                    for j in range(TC):
                        wait_before(dve, aggr_done, NTILE, stats2_done, TC * c + j + 1)
                        dve.bn_aggr(mv2[:, j], stats2[:, j]).then_inc(aggr2_done, 1)
                elif kind == "norm":
                    dve.wait_ge(aggr2_done, TC * c + TC)
                    dve.wait_ge(rstd2_done, c + 1)
                    for j in range(TC):
                        dve.tensor_scalar(xn2[:, j], h_tok[:, bass.ds(TC * c + j, 1), :].rearrange("p a d -> p (a d)"),
                                          mv2[:, j, 0:1], rstd2[:, j:j + 1],
                                          ALU.subtract, ALU.mult).then_inc(xn2_done, 1)
                elif kind == "x":
                    dve.wait_ge(x2Th_done, 2 * c + n + 1)
                    dve.tensor_tensor(chunk_tiles(xnT_l, c, n),
                                      bank_of(c, step)[:, 0:N].rearrange("p (j k t) -> p j k t", j=2, k=DT),
                                      chunk_tiles(xnT_h, c, n).bitcast(F32), ALU.subtract).then_inc(emptied[place(c, step)[0]], 1)

            links = [0]

            def router(c, part):
                f = c - 1
                n = links
                sc4 = score[:].rearrange("p j (g s) -> p (j g) s", s=GS)

                def link(ins, before_max=False):
                    ins.then_inc(route_step, 1)
                    n[0] += 1
                    if before_max:
                        wait_before(dve, aggr_done, NTILE, route_step, f * STEPS + (K0 + n[0]))
                    else:
                        dve.wait_ge(route_step, f * STEPS + (K0 + n[0]))

                if part == 0:
                    n[0] = 0
                    bank, before = job_number(c, -1)
                    dve.wait_ge(emptied[bank], before + 1)
                    link(dve.tensor_scalar(en[:], en[:], 1.0, None, ALU.add))
                    link(dve.reciprocal(score[:], en[:]))
                    at = 0
                    for d in range(1, GS):
                        ins = dve.tensor_tensor(gsum6[:, :, at:at + GS - d], sc4[:, :, 0:GS - d], sc4[:, :, d:GS], ALU.add)
                        at += GS - d
                        link(ins)
                    link(dve.tensor_reduce(gsum[:].rearrange("p j g -> p (j g)"), gsum6[:], AX.X, ALU.max))
                elif part == 1:
                    rival = gsum[:, :, None, :].to_broadcast([TT, TC, N_GROUP, N_GROUP])
                    own = gsum[:, :, :, None].to_broadcast([TT, TC, N_GROUP, N_GROUP])
                    dve.tensor_tensor(g_gt[:], rival, own, ALU.is_gt)
                    link(dve.tensor_tensor(g_ge[:], rival, own, ALU.is_equal))
                    link(dve.tensor_tensor(g_ge[:], g_ge[:], lower[:, None].to_broadcast([TT, TC, N_GROUP, N_GROUP]), ALU.mult))
                    link(dve.tensor_tensor(g_gt[:], g_gt[:], g_ge[:], ALU.add))
                    link(dve.tensor_reduce(g_rank[:].rearrange("p j g -> p (j g)"),
                                           g_gt[:].rearrange("p j g r -> p (j g) r"), AX.X, ALU.add))
                    link(dve.tensor_scalar(g_in[:], g_rank[:], 1.5, None, ALU.is_lt))
                    link(dve.tensor_tensor(masked[:].rearrange("p j (g s) -> p (j g) s", s=GS), sc4,
                                           g_in[:].rearrange("p j g -> p (j g)")[:, :, None].to_broadcast([TT, TC * N_GROUP, GS]),
                                           ALU.mult), before_max=True)
                elif part == 2:
                    for j in range(TC):
                        ins = dve.max(top8[:, j], masked[:, j])
                    link(ins)
                    kth = top8[:, :, TOP_K - 1:TOP_K].to_broadcast([TT, TC, E])
                    dve.tensor_tensor(above[:], masked[:], kth, ALU.is_gt)
                    dve.tensor_tensor(equal[:], masked[:], kth, ALU.is_equal)
                    link(dve.tensor_tensor(run[0][:, :, PAD:], masked[:], kth, ALU.is_equal))
                    link(dve.tensor_reduce(n_above[:], above[:], AX.X, ALU.add))
                    for s in range(4):
                        a, b = run[s % 2], run[1 - s % 2]
                        link(dve.tensor_tensor(b[:, :, PAD:], a[:, :, PAD:], a[:, :, PAD - (1 << s):PAD - (1 << s) + E], ALU.add))
                    link(dve.tensor_tensor(run[1][:, :, PAD:], run[0][:, :, PAD:],
                                           n_above[:, :, None].to_broadcast([TT, TC, E]), ALU.add))
                elif part == 3:
                    link(dve.tensor_scalar(run[1][:, :, PAD:], run[1][:, :, PAD:], TOP_K + 0.5, None, ALU.is_lt))
                    link(dve.tensor_tensor(taken[:], run[1][:, :, PAD:], equal[:], ALU.mult))
                    link(dve.tensor_tensor(taken[:], taken[:], above[:], ALU.add))
                    link(dve.tensor_tensor(taken[:], taken[:], score[:], ALU.mult))
                    link(dve.tensor_reduce(wsum[:], taken[:], AX.X, ALU.add))
                    link(dve.tensor_scalar(wsum[:], wsum[:], 1e-20, None, ALU.add))
                    link(dve.reciprocal(wrec[:], wsum[:]))
                    link(dve.scalar_tensor_tensor(out=comb[:], in0=taken[:], scalar=0.5 * ROUTED,
                                                  in1=wrec[:, :, None].to_broadcast([TT, TC, E]), op0=ALU.mult, op1=ALU.mult))
                    assert n[0] == STEPS, n[0]
                    dve.tensor_copy(comb_r[:], comb[:]).then_inc(comb_done, 1)
                    dve.wait_ge(comb_done, 3 * f + 1)
                    dve.tensor_copy(comb2[:, :, 0], comb_r[:].bitcast(F32)).then_inc(comb_done, 1)
                    dve.tensor_tensor(comb2[:, :, 1], comb[:], comb_r[:].bitcast(F32), ALU.subtract).then_inc(comb_done, 1)

            def experts(c, k):
                f = c - 1
                if k < NU:
                    dve.wait_ge(tanh_done, NU * f + k + 1)
                    if k >= 2:
                        dve.wait_ge(gl_done, NU * f + k - 1)
                    gate = g2 if k < NSH else g1
                    ins = dve.scalar_tensor_tensor(out=gate[:, k % 2], in0=th[:, k % 2], scalar=1.0,
                                                   in1=ps[:, 2 + k % 2, 0:N], op0=ALU.add, op1=ALU.mult)
                    if k < NSH:
                        ins.then_inc(g2_done, 1)
                    else:
                        ins.then_inc(g1_done, 1)
                        dve.wait_ge(g1_done, E * f + k - NSH + 1)
                        dve.wait_ge(w_ps, E * f + k - NSH + 1)
                        dve.tensor_tensor(g2[:, k % 2], g1[:, k % 2], ps[:, 4, 0:N], ALU.mult).then_inc(g2_done, 1)
                for part in ROUTE.get(k, []):
                    router(c, part)
                if k == NSH - 1:
                    wait_filled(dve, c, "combT")
                    dve.tensor_copy(combT[:], bank_of(c, "combT")[0:2 * E, 0:N]).then_inc(emptied[place(c, "combT")[0]], 1)

            def finish(c):
                dve.wait_ge(res_free, 16 * c)
                for j in range(TC):
                    wait_filled(dve, c, f"f{j}")
                    dve.tensor_tensor(res[:, j], bank_of(c, f"f{j}")[0:TT, 0:D],
                                      h_tok[:, bass.ds(TC * (c - 1) + j, 1), :].rearrange("p a d -> p (a d)"),
                                      ALU.add).then_inc(emptied[place(c, f"f{j}")[0]], 1)
                wait_emptied(dve, c, f"f{TC - 1}")
                dve.engine_nop().then_inc(res_done, TC)

            def body(c, has_attention=True, has_experts=True):
                if not has_experts:
                    for step in FIRST_STEPS:
                        attention(c, step)
                if has_experts:
                    for part in ROUTE[-1]:
                        router(c, part)
                if not has_experts:
                    for step in TOK_PLAN.get(-1, []):
                        tokens(*step)
                for k in range(SLOTS):
                    if not has_experts and k == CONSTANTS_SLOT:
                        chunk_constants()
                    if has_experts:
                        experts(c, k)
                    for step in TOK_PLAN.get(k, []) if not has_experts else []:
                        tokens(*step)
                    if has_attention:
                        for step in steps(c, k):
                            attention(c, step)
                    for n in UNIT_PLAN.get(k, []) if not has_experts else []:
                        if n % 2:
                            unit_low(dve, n)
                if has_experts:
                    finish(c)
                if has_attention:
                    for step in LAST_STEPS:
                        attention(c, step)

            body(0, has_experts=False)
            with dve.Fori(1, NC - 1) as c:
                body(c)
            body(NC - 1)
            body(NC, has_attention=False)

        @block.tensor
        def _(pe):
            def turn_patches(n):
                pe.wait_ge(grouped, n + 1)
                if n >= 2:
                    pe.wait_ge(patch_l, n - 1)
                for w in range(NW):
                    mm = pe.transpose(ps[:, 2 + n % 2, w * RC:(w + 1) * RC], xp[:, n % XP, w], ident[0:RC, 0:RC])
                mm.then_inc(patch_ps, 1)

            def embed(n):
                c, k = divmod(n, KT)
                pe.wait_ge(tokw_done, 1 if n < KT // 2 else 2)
                pe.wait_ge(patch_l, n + 1)
                if k == 0 and c:
                    pe.wait_ge(emb_sb, DT * c)
                for dt in range(DT):
                    for i, (a, b) in enumerate(((tokw_h, pt_h), (tokw_h, pt_l), (tokw_l, pt_h))):
                        mm = pe.matmul(ps[:, dt, 0:NP], a[:, k, dt * 128:(dt + 1) * 128], b[:, n % PS],
                                       start=(k == 0 and i == 0), stop=(k == KT - 1 and i == 2))
                mm.then_inc(patch_used, 1)

            def turn_signs(n):
                m, ot = divmod(n, DT)
                pe.wait_ge(signs_done, m + 1)
                if n >= 3:
                    pe.wait_ge(signT_done, n - 2)
                for kt in range(DT):
                    mm = pe.transpose(ps[:, 5 + n % 3, kt * 128:(kt + 1) * 128], wsign[:, m, ot, kt * 128:(kt + 1) * 128], ident[:])
                mm.then_inc(signT_ps, 1)

            def turn_gate():
                pe.wait_ge(ld_gate, 16)
                pe.wait_ge(signT_done, NTURN - 2)
                for kt in range(DT):
                    mm = pe.transpose(ps[:, 5 + NTURN % 3, kt * E:(kt + 1) * E], gate_w[:, kt * 128:(kt + 1) * 128], ident[0:E, 0:E])
                mm.then_inc(gateT_ps, 1)

            def tokens(c, kind, n):
                if kind == "piece":
                    n = c * KT + n
                    if n + 2 < NC * KT:
                        turn_patches(n + 2)
                    embed(n)
                elif kind == "signT":
                    turn_signs(2 * n)
                    turn_signs(2 * n + 1)
                elif kind == "gateT":
                    turn_gate()
                elif kind == "tok":
                    if n == 0:
                        pe.wait_ge(cls_done, 2 * DT)
                        pe.wait_ge(emb_sb, DT * (c + 1))
                        if c:
                            pe.wait_ge(xnTl_done, 2 * c)
                    else:
                        pe.wait_ge(tok_sb, 2 * c + 1)
                    for j in range(2):
                        for dt in range(DT):
                            src = hT[:, c % 2, dt].rearrange("p b t -> p (b t)")[:, (2 * n + j) * TT:(2 * n + j + 1) * TT]
                            mm = pe.transpose(ps[0:TT, 4, j * D + dt * 128:j * D + (dt + 1) * 128], src, ident[:])
                    mm.then_inc(tok_ps, 1)
                elif kind == "turn":
                    if n == 0:
                        pe.wait_ge(tok_sb, 2 * c + 2)
                        pe.wait_ge(xn_done, TC * c + TC)
                    else:
                        pe.wait_ge(xnTl_done, 2 * c + 1)
                    for j in range(2):
                        for kt in range(DT):
                            at = (j * DT + kt) * TT
                            mm = pe.transpose(ps[:, 4, at:at + TT], xn[:, 2 * n + j, kt * 128:(kt + 1) * 128], ident[0:TT, 0:TT])
                    mm.then_inc(xnT_ps, 1)

            pe.wait_ge(pool_const, 2)
            turn_patches(0)
            turn_patches(1)
            for step in PROLOGUE:
                tokens(*step)
            pe.wait_ge(xnTl_done, 2)
            pe.wait_ge(gateT_done, 1)
            pe.wait_ge(signT_done, NTURN)

            def is_first(c):
                return isinstance(c, int) and c == 0

            def start(c, job, made_of=()):
                bank, before = place(c, job)
                wait_all_emptied(pe, c, [source for source in made_of if place(c, source)[0] != bank])
                pe.wait_ge(emptied[bank], before)
                return bank_of(c, job)

            def attention(c, step):
                kind, n = step.rstrip("0123456789"), int(step[-1]) if step[-1].isdigit() else 0
                if kind in ("qkv", "next"):
                    m, mt = divmod(n, DT)
                    tokens = bass.ds(N * c, N) if kind == "qkv" else bass.ds(N * c + N, N)
                    out_ps = start(c, step)
                    for kt in range(DT):
                        for i, b in enumerate((xnT_h, xnT_l)):
                            mm = pe.matmul(out_ps[:, 0:N], signT[:, m, kt, mt * 128:(mt + 1) * 128],
                                           b[:, kt, tokens], start=(kt == 0 and i == 0),
                                           stop=(kt == DT - 1 and i == 1))
                    mm.then_inc(filled[place(c, step)[0]], 1)
                elif kind == "v":
                    out_ps = start(c, step, ["qkv4", "qkv5"] if n == 0 and is_first(c) else [])
                    for mt in range(DT):
                        mm = pe.transpose(out_ps[0:TT, mt * 128:(mt + 1) * 128], vT[:, mt, n * TT:(n + 1) * TT], ident[:])
                    mm.then_inc(filled[place(c, step)[0]], 1)
                elif kind in "sz":
                    qk = [f"qkv{i}" for i in range(2 * DT)] if n == 0 and kind == "s" and is_first(c) else []
                    step = f"s{n}"
                    banks = ([start(c, step + "a", qk), start(c, step + "b")] if kind == "s"
                             else [bank_of(c, step + "a"), bank_of(c, step + "b")])
                    if kind == "z":
                        pe.wait_ge(scores_half, 2 * (TC * c + n + 1))
                    for mt in range(DT):
                        for i in range(2):
                            for r in (0, 1) if kind == "s" else (2, 3):
                                rows = slice(32 * r, 32 * r + 32)
                                img = 2 * n + i
                                at = (r // 2 * DT + mt) * TT + i * T
                                mm = pe.matmul(banks[r % 2][0:TT, at:at + T],
                                               qblk[rows, mt, img].rearrange("p a t -> p (a t)"),
                                               kT[rows, mt, img * T:(img + 1) * T], start=True, stop=True)
                                if (mt, i) == (DT - 1, 1):
                                    mm.then_inc(scores_half if kind == "s" else filled[place(c, step + "ab"[r % 2])[0]], 1)
                elif kind == "t":
                    pe.wait_ge(p_done, TC * c + n + 1)
                    for mt in range(DT):
                        job = step + "ab"[mt]
                        out_ps = start(c, job)
                        for r in range(PPM):
                            mm = pe.transpose(out_ps[0:TT, r * TT:(r + 1) * TT],
                                              probs[:, n % 2, r % 2, r // 2, mt].rearrange("p i s -> p (i s)"), ident[0:TT, 0:TT])
                        mm.then_inc(filled[place(c, job)[0]], 1)
                elif kind == "y":
                    for mt in range(DT):
                        job = step + "ab"[mt]
                        out_ps = start(c, job, [f"v{j}" for j in range(TC)] * (n == 0) + [f"t{n}" + "ab"[mt]])
                        for h in range(2 * PPM):
                            mm = pe.matmul(out_ps[0:T, h * 2 * VC:(h + 1) * 2 * VC],
                                           probsT[:, n % 2, mt, h // 2, h % 2 * T:(h % 2 + 1) * T],
                                           vx[:, n, mt * 2 * PPM + h].rearrange("p i v -> p (i v)"),
                                           start=True, stop=True)
                        mm.then_inc(filled[place(c, job)[0]], 1)
                elif kind == "yT":
                    wait_all_emptied(pe, c, [f"y{j}{p}" for j in (2 * n, 2 * n + 1) for p in "ab"])
                    bank, before = place(c, step)
                    wait_before(pe, pool_const, 2, emptied[bank], before)
                    for j in range(2):
                        for mt in range(DT):
                            for i in range(2):
                                at = (j * DT + mt) * TT + i * T
                                mm = pe.transpose(bank_of(c, step)[:, at:at + T],
                                                  y[:, 2 * n + j, i, mt * 128:(mt + 1) * 128], ident[0:T, 0:T])
                    mm.then_inc(filled[place(c, step)[0]], 1)
                elif kind == "proj":
                    out_ps = start(c, step, ["yT0", "yT1"] if n == 0 else [])
                    for kt in range(DT):
                        for i, b in enumerate((yT_h, yT_l)):
                            mm = pe.matmul(out_ps[:, 0:N], signT[:, 3, kt, n * 128:(n + 1) * 128], b[:, kt],
                                           start=(kt == 0 and i == 0), stop=(kt == DT - 1 and i == 1))
                    mm.then_inc(filled[place(c, step)[0]], 1)
                elif kind == "h":
                    out_ps = start(c, step, ["proj0", "proj1"] if n == 0 else [])
                    for ot in range(DT):
                        mm = pe.transpose(out_ps[0:TT, ot * 128:(ot + 1) * 128], attnT[:, ot, n * TT:(n + 1) * TT], ident[:])
                    mm.then_inc(filled[place(c, step)[0]], 1)
                elif kind == "x":
                    pe.wait_ge(xn2_done, TC * c + 2 * n + 2)
                    out_ps = start(c, step)
                    for j in range(2):
                        for kt in range(DT):
                            at = (j * DT + kt) * TT
                            mm = pe.transpose(out_ps[:, at:at + TT], xn2[:, 2 * n + j, kt * 128:(kt + 1) * 128],
                                              ident[0:TT, 0:TT])
                    mm.then_inc(filled[place(c, step)[0]], 1)

                elif kind == "logitT":
                    bank, before = place(c, step)
                    wait_all_emptied(pe, c, ["x0", "x1"])
                    wait_before(pe, pool_const, 2, emptied[bank], before)
                    out_ps = bank_of(c, step)
                    for kt in range(DT):
                        for i, (a, b) in enumerate(((gate_h, xnT_h), (gate_h, xnT_l), (gate_l, xnT_h))):
                            mm = pe.matmul(out_ps[0:E, 0:N], a[:, kt], b[:, kt, bass.ds(N * c, N)],
                                           start=(kt == 0 and i == 0), stop=(kt == DT - 1 and i == 2))
                    mm.then_inc(filled[place(c, step)[0]], 1)
                elif kind == "logit":
                    wait_emptied(pe, c, "logitT")
                    bank, before = place(c, step)
                    wait_before(pe, pool_const, 2, emptied[bank], before)
                    for j in range(TC):
                        mm = pe.transpose(bank_of(c, step)[0:TT, j * E:(j + 1) * E], logitT[:, j * TT:(j + 1) * TT],
                                          ident[0:E, 0:E])
                    mm.then_inc(filled[bank], 1)

            def experts(c, k):
                f = c - 1
                tokens = bass.ds(N * f, N)
                if k < NU:
                    if k >= 2:
                        wait_gate(pe, f, k - 2)
                    for kt in range(DT):
                        for i, (a, b) in enumerate(((up_h, xnT_h), (up_h, xnT_l), (up_l, xnT_h))):
                            mm = pe.matmul(ps[:, 2 + k % 2, 0:N], a[:, k, kt], b[:, kt, tokens],
                                           start=(kt == 0 and i == 0), stop=(kt == DT - 1 and i == 2))
                    mm.then_inc(u_ps, 1)
                if k == NSH - 1:
                    pe.wait_ge(comb_done, 3 * f + 3)
                    out_ps = start(c, "combT")
                    for j in range(TC):
                        mm = pe.transpose(out_ps[0:2 * E, j * TT:(j + 1) * TT],
                                          comb2[:, j].rearrange("p a e -> p (a e)"), ident[0:TT, 0:TT])
                    mm.then_inc(filled[place(c, "combT")[0]], 1)
                if k >= 2:
                    u = k - 2
                    pe.wait_ge(gl_done, NU * f + u + 1)
                    for dt in range(DT):
                        w = slice(dt * 128, (dt + 1) * 128)
                        for i, (a, b) in enumerate(((dn_h, g_h), (dn_h, g_l), (dn_l, g_h))):
                            mm = pe.matmul(ps[:, dt, 0:N], a[:, u, w], b[:, u % GR],
                                           start=(u == 0 and i == 0), stop=(u == NU - 1 and i == 2))
                    mm.then_inc(dn_used, 1)
                if NSH <= k < NU:
                    e = k - NSH
                    if e == 0:
                        wait_emptied(pe, c, "combT")
                    else:
                        pe.wait_ge(g2_done, NU * f + k)
                    pe.matmul(ps[:, 4, 0:N], pick_r[:, e], combT[:], start=True, stop=True).then_inc(w_ps, 1)

            def body(c, has_attention=True, has_experts=True):
                if not has_experts:
                    for step in FIRST_STEPS:
                        attention(c, step)
                if not has_experts:
                    for step in TOK_PLAN.get(-1, []):
                        tokens(*step)
                for k in range(SLOTS):
                    if has_experts:
                        experts(c, k)
                    for step in TOK_PLAN.get(k, []) if not has_experts else []:
                        tokens(*step)
                    if has_attention:
                        for step in steps(c, k):
                            attention(c, step)
                if has_experts:
                    pe.wait_ge(ffn_sb, c)
                    for j in range(TC):
                        out_ps = start(c, f"f{j}")
                        for dt in range(DT):
                            mm = pe.transpose(out_ps[0:TT, dt * 128:(dt + 1) * 128], ffnT[:, dt, j * TT:(j + 1) * TT], ident[:])
                        mm.then_inc(filled[place(c, f"f{j}")[0]], 1)
                if has_attention:
                    for step in LAST_STEPS:
                        attention(c, step)

            body(0, has_experts=False)
            wait_all_emptied(pe, 0, [f"next{i}" for i in range(3 * DT)])
            pe.wait_ge(unit_l[0], NG)
            pe.wait_ge(unit_l[1], NG)
            pe.wait_ge(xnTl_done, 2 * NC)
            with pe.Fori(1, NC - 1) as c:
                body(c)
            body(NC - 1)
            body(NC, has_attention=False)


_INS = ["x", "cls_tok", "L0_tok_W", "L0_tok_b", "L0_attn_Wq", "L0_attn_bq", "L0_attn_Wk", "L0_attn_bk",
        "L0_attn_Wv", "L0_attn_bv", "L0_attn_Wp", "L0_attn_bp", "L0_ffn_gate_weight", "L0_ffn_expert_up",
        "L0_ffn_expert_down", "L0_ffn_shared_up", "L0_ffn_shared_down"]


def kernel(**inputs):
    import concourse.bacc as bacc
    from concourse.bass_utils import run_bass_kernel_spmd

    nc = bacc.Bacc("TRN2", target_bir_lowering=False, num_devices=1)
    arrays, args = {}, []
    for name in _INS:
        a = np.ascontiguousarray(inputs[name])
        arrays[f"in_{name}"] = a
        args.append(nc.dram_tensor(f"in_{name}", a.shape, F32, kind="ExternalInput").ap())
    B, _, H, W = inputs["x"].shape
    D = inputs["L0_tok_W"].shape[1]
    shape = (B, (H // 16) * (W // 16) + 1, D)
    args.append(nc.dram_tensor("out_h", shape, F32, kind="ExternalOutput").ap())
    vit_block(nc, *args)
    r = run_bass_kernel_spmd(nc, [arrays], core_ids=[0])
    return r.results[0]["out_h"]
```
